# Optimizing a Trainium2 kernel written in Bass

```python
import numpy as np
import jax
import jax.numpy as jnp

def _softmax(x, axis=-1):
    return jax.nn.softmax(x, axis=axis)

def _gelu(x):
    return jax.nn.gelu(x, approximate=True)

def _silu(x):
    return jax.nn.silu(x)

def _sigmoid(x):
    return jax.nn.sigmoid(x)

def _layernorm(x, axis=-1, eps=1e-05):
    m = jnp.mean(x, axis=axis, keepdims=True)
    v = jnp.var(x, axis=axis, keepdims=True)
    return (x - m) / jnp.sqrt(v + eps)

def _scatter_add(tgt, idx, src, axis=0):
    return tgt.at[idx].add(src)

def _segment_sum(src, seg, n):
    return jax.ops.segment_sum(src, seg, n)
kernel_name = 'mk_adaln_d1_jaxref_r8_658952'

def setup_inputs(seed: int=0):
    np.random.seed(seed)
    _w = jnp.asarray

    def _L0_attn_setup():
        import jax, jax.numpy as jnp
        import numpy as np
        D = 128
        key = jax.random.key(seed)
        k0, k1, k2, k3 = jax.random.split(key, 4)
        x = jax.random.normal(k0, (4, 256, D), dtype=jnp.float32)
        Wk = jax.random.normal(k1, (D, D), dtype=jnp.float32) * 0.02
        Wq = jax.random.normal(k2, (D, D), dtype=jnp.float32) * 0.02
        Wv = jax.random.normal(k3, (D, D), dtype=jnp.float32) * 0.02
        return {'x': x, 'Wk': Wk, 'Wq': Wq, 'Wv': Wv}
    _L0_attn_in = _L0_attn_setup()

    def _L0_ffn_setup():
        import jax, jax.numpy as jnp
        import numpy as np
        B, S, H, E, K = (2, 128, 128, 8, 2)
        F = 4 * H
        key = jax.random.key(seed)
        ks = jax.random.split(key, 8)
        std = 0.02
        return {'x': jax.random.normal(ks[0], (B, S, H), jnp.float32), 'gate_w': jax.random.normal(ks[1], (E, H), jnp.float32) * (std / np.sqrt(H)), 'gate_bias': jnp.zeros((E,), jnp.float32), 'Wu': jax.random.normal(ks[2], (E, F, H), jnp.float32) * std, 'bu': jnp.zeros((E, F), jnp.float32), 'Wd': jax.random.normal(ks[3], (E, H, F), jnp.float32) * std, 'bd': jnp.zeros((E, H), jnp.float32), 'sWu': jax.random.normal(ks[4], (F, H), jnp.float32) * std, 'sbu': jnp.zeros((F,), jnp.float32), 'sWd': jax.random.normal(ks[5], (H, F), jnp.float32) * std, 'sbd': jnp.zeros((H,), jnp.float32)}
    _L0_ffn_in = _L0_ffn_setup()
    _L0_c = _w((lambda *s: np.random.randn(*s).astype(np.float32) * 0.05)(2, 128))
    _L0_wmod = _w((lambda *s: np.random.randn(*s).astype(np.float32) * 0.05)(128, 6 * 128) * 128 ** (-0.5))
    _d = {'L0_attn_x': _L0_attn_in['x'], 'L0_attn_Wk': _L0_attn_in['Wk'], 'L0_attn_Wq': _L0_attn_in['Wq'], 'L0_attn_Wv': _L0_attn_in['Wv'], 'L0_ffn_gate_w': _L0_ffn_in['gate_w'], 'L0_ffn_gate_bias': _L0_ffn_in['gate_bias'], 'L0_ffn_Wu': _L0_ffn_in['Wu'], 'L0_ffn_bu': _L0_ffn_in['bu'], 'L0_ffn_Wd': _L0_ffn_in['Wd'], 'L0_ffn_bd': _L0_ffn_in['bd'], 'L0_ffn_sWu': _L0_ffn_in['sWu'], 'L0_ffn_sbu': _L0_ffn_in['sbu'], 'L0_ffn_sWd': _L0_ffn_in['sWd'], 'L0_ffn_sbd': _L0_ffn_in['sbd'], 'L0_c': _L0_c, 'L0_wmod': _L0_wmod}
    _x0 = _d['L0_attn_x']
    _d['L0_attn_x'] = jax.random.normal(jax.random.fold_in(jax.random.key(seed), 1), (2, 2048, 128), dtype=_x0.dtype)
    del _x0
    return _d

def reference(L0_attn_x, L0_attn_Wk, L0_attn_Wq, L0_attn_Wv, L0_ffn_gate_w, L0_ffn_gate_bias, L0_ffn_Wu, L0_ffn_bu, L0_ffn_Wd, L0_ffn_bd, L0_ffn_sWu, L0_ffn_sbu, L0_ffn_sWd, L0_ffn_sbd, L0_c, L0_wmod):

    def _L0_attn_ref(x, Wk, Wq, Wv):
        import jax, jax.numpy as jnp
        import numpy as np
        D = 128
        K = x @ Wk
        Q = x @ Wq
        V = x @ Wv
        N = Q.shape[-2]
        d = K.shape[-1]
        scores = jnp.einsum('bnd,bmd->bnm', Q, K) / jnp.sqrt(jnp.float32(d))
        causal = jnp.tril(jnp.ones((N, N), dtype=bool))
        scores = jnp.where(causal[None, :, :], scores, -jnp.inf)
        attn = jax.nn.softmax(scores, axis=-1)
        return attn @ V

    def _L0_ffn_ref(x, gate_w, gate_bias, Wu, bu, Wd, bd, sWu, sbu, sWd, sbd):
        import jax, jax.numpy as jnp
        import numpy as np
        B, S, H, E, K = (2, 128, 128, 8, 2)
        F = 4 * H
        b, s, h = x.shape
        x_flat = x.reshape(-1, h)
        T = x_flat.shape[0]
        scores = jax.nn.sigmoid(x_flat @ gate_w.T + gate_bias)
        top_scores, top_idx = jax.lax.top_k(scores, K)
        top_scores = top_scores / (top_scores.sum(-1, keepdims=True) + 1e-06)
        w = jnp.zeros((T, E), x.dtype).at[jnp.arange(T)[:, None], top_idx].add(top_scores)
        h1 = jnp.einsum('th,efh->etf', x_flat, Wu) + bu[:, None, :]
        a1 = jax.nn.gelu(h1, approximate=False)
        y = jnp.einsum('etf,ehf->eth', a1, Wd) + bd[:, None, :]
        combined = jnp.einsum('te,eth->th', w, y)
        sh = jax.nn.gelu(x_flat @ sWu.T + sbu, approximate=False)
        shared = (sh @ sWd.T + sbd) * 0.1
        return (combined + shared).reshape(b, s, h)
    x = L0_attn_x
    mod = (_silu(L0_c) @ L0_wmod).reshape(L0_c.shape[0], 6, 1, -1)
    sa, ca, ga, sb, cb, gb = (mod[:, 0], mod[:, 1], mod[:, 2], mod[:, 3], mod[:, 4], mod[:, 5])
    ga = (2 * (ga >= 0) - 1) * jnp.maximum(jnp.abs(ga), 0.25)
    gb = (2 * (gb >= 0) - 1) * jnp.maximum(jnp.abs(gb), 0.25)
    h = _layernorm(x, axis=-1) * (1 + ca) + sa
    x = x + ga * _L0_attn_ref(h, L0_attn_Wk, L0_attn_Wq, L0_attn_Wv)
    h = _layernorm(x, axis=-1) * (1 + cb) + sb
    x = x + gb * _L0_ffn_ref(h, L0_ffn_gate_w, L0_ffn_gate_bias, L0_ffn_Wu, L0_ffn_bu, L0_ffn_Wd, L0_ffn_bd, L0_ffn_sWu, L0_ffn_sbu, L0_ffn_sWd, L0_ffn_sbd)
    return x

_drawn_inputs = setup_inputs


def setup_inputs(seed=0):
    import zlib

    import numpy as np

    out = dict(_drawn_inputs(seed))
    spreads = {'L0_ffn_gate_bias': (0.0, 0.352),
     'L0_ffn_bu': (0.0, 0.8),
     'L0_ffn_bd': (0.0, 0.467),
     'L0_ffn_sbu': (0.0, 0.8),
     'L0_ffn_sbd': (0.0, 2.0)}
    factors = {'L0_attn_Wk': 8.0,
     'L0_attn_Wq': 8.0,
     'L0_attn_Wv': 8.0,
     'L0_ffn_gate_w': 5.202,
     'L0_ffn_Wu': 6.016,
     'L0_ffn_Wd': 5.437,
     'L0_ffn_sWu': 8.0,
     'L0_ffn_sWd': 8.0,
     'L0_c': 2.695,
     'L0_wmod': 2.765}
    for name, (base, spread) in spreads.items():
        noise = np.random.default_rng([zlib.crc32(name.encode()), seed]).standard_normal(out[name].shape)
        drawn = base * np.exp(spread * noise) if base else spread * noise
        out[name] = jnp.asarray(drawn.astype(out[name].dtype))
    for name, factor in factors.items():
        out[name] = (out[name] * factor).astype(out[name].dtype)
    return out
```

```python
from contextlib import ExitStack

import concourse.bass as bass
from concourse import mybir

ALU = mybir.AluOpType
ACT = mybir.ActivationFunctionType
F32 = mybir.dt.float32
F32R = mybir.dt.float32r
AX_X = mybir.AxisListType.X

P = 128
BLOCK = 512
TPB = BLOCK // P
MASKED = -1.0e30
LN_EPS = 1e-5



class Steps:

    def __init__(self, base=0):
        self.base, self.n = base, 0

    def next(self):
        self.n += 1
        return self.base + self.n


def adaln_attention_moe(nc, x, Wk, Wq, Wv, gate_w, gate_bias, Wu, bu, Wd, bd, sWu, sbu, sWd, sbd, c, wmod, out):
    NB, SEQ, D = x.shape
    E, F, _ = Wu.shape
    assert D == P and SEQ % BLOCK == 0 and F % P == 0
    NT = SEQ // P
    NQ = SEQ // BLOCK
    TILES = NB * NT
    FC = F // P
    SLOTS = E + 1
    NBLK = NB * NQ
    SCALE = float(D) ** -0.5

    CHUNK = [0]
    for i in range(NT):
        CHUNK.append(CHUNK[-1] + i // TPB + 1)
    NCH = CHUNK[NT]

    def chunks(i):
        return range(i // TPB + 1)

    def key_tiles(i, k):
        return TPB if k < i // TPB else i % TPB + 1

    RING = 5
    NPROJ = 3 * NQ

    turn = [("x", q, 0) for q in range(NQ)]
    for i in range(NT + 1):
        if i % TPB == 1 and i > 1:
            turn.append(("o", i // TPB - 1, 0))
        if i > 0:
            turn += [("p", i - 1, k) for k in chunks(i - 1)]
    turn.append(("o", NQ - 1, 0))
    TURN = {item: n for n, item in enumerate(turn)}
    assert len(turn) % 2 == 0

    ROW_BU, ROW_BD = 0, SLOTS * FC
    ROW_GATE = ROW_BD + SLOTS
    ROW_C = ROW_GATE + E
    ROWS = ROW_C + NB
    assert ROWS <= P
    SA, CA, GA, SB, CB, GB = range(6)

    w_dram = nc.dram_tensor("route_scratch", (NB, NT, E, P), F32, kind="Internal").ap()

    with ExitStack() as ctx:
        def sb(name, shape, dt=F32):
            return ctx.enter_context(nc.sbuf_tensor(name, shape, dt))

        def sem(name):
            return ctx.enter_context(nc.semaphore(name))

        bank = [ctx.enter_context(nc.psum_tensor(f"bank{i}", [P, BLOCK], F32)) for i in range(8)]

        ident = sb("ident", [P, P])
        ident_r = sb("ident_r", [P, P], F32R)
        mask = sb("mask", [P, P])
        mask_r = sb("mask_r", [P, P], F32R)
        rows = sb("rows", [P, P])
        cols = sb("cols", [P, ROWS])
        gate_b = sb("gate_b", [P, E])
        down_count = sb("down_count", [P, E])
        silu = sb("silu", [P, 4, NB])
        wmod_sb = sb("wmod_sb", [P, 6 * P])
        mods = sb("mods", [P, 6 * NB])
        mod_now = sb("mod_now", [P, 6])
        bias_now = sb("bias_now", [P, 2, FC])
        gsign = sb("gsign", [P, NB])
        wqkv = sb("wqkv", [P, 3 * P])
        wqkv_hi = sb("wqkv_hi", [P, 3 * P], F32R)
        wqkv_lo = sb("wqkv_lo", [P, 3 * P], F32R)
        x_sb = sb("x_sb", [P, TILES * P])
        bn = sb("bn", [P, TILES, 6])
        mean = sb("mean", [P, TILES])
        var = sb("var", [P, TILES])
        std = sb("std", [P, TILES])
        rstd = sb("rstd", [P, TILES])
        newton = sb("newton", [P, TILES])
        xn = sb("xn", [P, 2, BLOCK])
        hT = sb("hT", [P, 2, BLOCK])
        hT_hi = sb("hT_hi", [P, 2, BLOCK], F32R)
        hT_lo = sb("hT_lo", [P, 2, BLOCK], F32R)
        qk_hi = sb("qk_hi", [P, 2 * SEQ], F32R)
        qk_lo = sb("qk_lo", [P, 2 * SEQ], F32R)
        v_sb = sb("v_sb", [P, SEQ])
        probs = sb("probs", [P, 2, SEQ])
        probsT = sb("probsT", [P, NT * BLOCK])
        chunk_max = sb("chunk_max", [P, 2, NQ])
        max_junk = sb("max_junk", [P, 2, NQ])
        neg_max = sb("neg_max", [P, NT])
        exp_sum = sb("exp_sum", [P, NT, NQ])
        row_sum = sb("row_sum", [P, TPB])
        row_inv = sb("row_inv", [P, TPB])
        oT = sb("oT", [P, 2, BLOCK])
        x1 = sb("x1", [P, 2, BLOCK])
        bn_now = sb("bn_now", [P, 2, TPB, 6])
        raw_up = sb("raw_up", [P, 2, FC * P])
        raw_down = sb("raw_down", [P, 2, F])
        up_hi = sb("up_hi", [P, 2, F], F32R)
        up_lo = sb("up_lo", [P, 2, F], F32R)
        down_hi = sb("down_hi", [P, 2, FC * P], F32R)
        down_lo = sb("down_lo", [P, 2, FC * P], F32R)
        a_hi = sb("a_hi", [P, 2, FC * BLOCK], F32R)
        a_lo = sb("a_lo", [P, 2, FC * BLOCK], F32R)
        logits = sb("logits", [P, TILES * E])
        score = sb("score", [P, TILES, E])
        tie = sb("tie", [P, TILES, E])
        pick1 = sb("pick1", [P, TILES, E])
        pick2 = sb("pick2", [P, TILES, E])
        best = sb("best", [P, 4, TILES])
        weight = sb("weight", [P, TILES * E])
        weightT = sb("weightT", [P, NB, P])

        a_sb = probs[:, :, :]
        assert SEQ == FC * BLOCK and NT * BLOCK >= 2 * TILES * P and NB == 2
        acc = probsT[:, 0:TILES * P]
        w_bc = probsT[:, TILES * P:2 * TILES * P].rearrange("p (b t) -> p b t", b=NB)
        h2_hi, h2_lo = qk_hi, qk_lo
        yw = x1

        x_in = [sem(f"x_in{b}_{h}") for b in range(NB) for h in range(2)]
        rows_in, qkv_in, wmod_in, gate_b_in = sem("rows_in"), sem("qkv_in"), sem("wmod_in"), sem("gate_b_in")
        raw_in = [sem("raw_in0"), sem("raw_in1")]
        pool_ready = sem("pool_ready")
        consts_r = sem("consts_r")
        rows_T, cols_ready = sem("rows_T"), sem("cols_ready")
        silu_exp, silu_ready, mod_mm, mods_ready = sem("silu_exp"), sem("silu_ready"), sem("mod_mm"), sem("mods_ready")
        var_ready, std_ready = sem("var_ready"), sem("std_ready")
        dve_step = sem("dve_step")
        xn_ready, xT_done = sem("xn_ready"), sem("xT_done")
        h_hi_done, h_lo_done = sem("h_hi_done"), sem("h_lo_done")
        proj_done, qk_hi_done, qk_lo_done, v_done = sem("proj_done"), sem("qk_hi_done"), sem("qk_lo_done"), sem("v_done")
        score_done, neg_max_ready, exp_done = sem("score_done"), sem("neg_max_ready"), sem("exp_done")
        pT_done, pT_act, pT_dve = sem("pT_done"), sem("pT_act"), sem("pT_dve")
        pv_done, oT_ready, oTT_done, x1_done = sem("pv_done"), sem("oT_ready"), sem("oTT_done"), sem("x1_done")
        x1_stats, x1_kept = sem("x1_stats"), sem("x1_kept")
        x2n_ready, x2T_done = sem("x2n_ready"), sem("x2T_done")
        h2_hi_done, h2_lo_done, gate_done, logit_ready = sem("h2_hi_done"), sem("h2_lo_done"), sem("gate_done"), sem("logit_ready")
        sig_exp, weight_ready, weightT_mm, weightT_ready, weight_out = sem("sig_exp"), sem("weight_ready"), sem("weightT_mm"), sem("weightT_ready"), sem("weight_out")
        w_bc_in = [sem("w_bc_in0"), sem("w_bc_in1")]
        wT_done, w_hi_done, w_lo_done = sem("wT_done"), sem("w_hi_done"), sem("w_lo_done")
        up_done, gelu_done, a_hi_done, a_lo_done = sem("up_done"), sem("gelu_done"), sem("a_hi_done"), sem("a_lo_done")
        START = 1
        down_done, yw_ready, acc_done = sem("down_done"), sem("yw_ready"), sem("acc_done")
        accg_ready, accT_done, out_ready, stored = sem("accg_ready"), sem("accT_done"), sem("out_ready"), sem("stored")

        x_tiles = x.rearrange("b (n p) d -> p b n d", p=P)
        out_tiles = out.rearrange("b (n p) d -> p b n d", p=P)
        x_view = x_sb[:, :].rearrange("p (b n d) -> p b n d", b=NB, n=NT)

        def tok(tile, n=1):
            return bass.ds(tile * P, n * P)

        def mod(j, b):
            return mods[:, j * NB + b:j * NB + b + 1]

        block = ctx.enter_context(nc.Block())

        @block.sync
        def _(sync):
            def load_raw(s, up, down):
                sync.dma_start(raw_up[:, s % 2, :].rearrange("p (f h) -> p f h", f=FC),
                               up.rearrange("(f p) h -> p f h", p=P)).then_inc(raw_in[s % 2], 16)
                sync.dma_start(raw_down[:, s % 2, :], down).then_inc(raw_in[s % 2], 16)

            half = NT // 2
            for b in range(NB):
                for h in range(2):
                    sync.dma_start(x_view[:, b, h * half:(h + 1) * half, :],
                                   x_tiles[:, b, h * half:(h + 1) * half, :]).then_inc(x_in[2 * b + h], 16)
            load_raw(0, sWu, sWd)
            load_raw(1, Wu[0], Wd[0])
            for s in (2, 3):
                sync.wait_ge(wT_done, 2 * (s - 2) + 2)
                load_raw(s, Wu[s - 1], Wd[s - 1])

            sync.wait_ge(weightT_ready, NB)
            sync.dma_start(w_dram.rearrange("b n e t -> (n e) b t"), weightT[:, :, :]).then_inc(weight_out, 16)
            sync.wait_ge(weight_out, 16)

            def load_weights_bc(s, e, b):
                sync.dma_start(w_bc[:, b, :].rearrange("p (n t) -> p n t", n=NT),
                               w_dram[b, :, e, :].rearrange("n (o t) -> o n t", o=1).broadcast_to([P, NT, P])
                               ).then_inc(w_bc_in[b], 16)

            for b in range(NB):
                load_weights_bc(1, 0, b)
            for s in range(2, SLOTS):
                if s + 2 < SLOTS:
                    sync.wait_ge(wT_done, 2 * s + 2)
                    load_raw(s + 2, Wu[s + 1], Wd[s + 1])
                for b in range(NB):
                    sync.wait_ge(yw_ready, START + NBLK * (s - 1) + NQ * (b + 1))
                    load_weights_bc(s, s - 1, b)

            for n in range(NBLK):
                b, q = n // NQ, n % NQ
                sync.wait_ge(out_ready, n + 1)
                sync.dma_start(out_tiles[:, b, TPB * q:TPB * (q + 1), :],
                               x_view[:, b, TPB * q:TPB * (q + 1), :]).then_inc(stored, 16)
            sync.wait_ge(stored, 16 * NBLK)

        @block.gpsimd
        def _(pool):
            pool.sem_inc(x1_kept, START)
            pool.sem_inc(acc_done, START)
            nc.gpsimd.memset(rows[:, :], 0.0).then_inc(pool_ready, 1)
            nc.gpsimd.memset(ident[:, :], 0.0).then_inc(pool_ready, 1)
            nc.gpsimd.memset(mask[:, :], 0.0).then_inc(pool_ready, 1)
            nc.gpsimd.iota(down_count[:, :], pattern=[[-1, E]], base=E, channel_multiplier=0,
                           allow_small_or_imprecise_dtypes=True).then_inc(pool_ready, 1)
            pool.wait_ge(pool_ready, 4)
            for at, src in ((ROW_BU, sbu.rearrange("(c f) -> c f", f=P)),
                            (ROW_BU + FC, bu.rearrange("e (c f) -> (e c) f", f=P)),
                            (ROW_BD, sbd.rearrange("(o h) -> o h", o=1)),
                            (ROW_BD + 1, bd), (ROW_GATE, gate_w), (ROW_C, c)):
                pool.dma_start(rows[at:at + src.shape[0], :], src).then_inc(rows_in, 16)
            pool.dma_start(wmod_sb[:, :], wmod).then_inc(wmod_in, 16)
            for j, w in enumerate((Wq, Wk, Wv)):
                pool.dma_start(wqkv[:, j * P:(j + 1) * P], w).then_inc(qkv_in, 16)
            pool.dma_start(gate_b[:, :], gate_bias.rearrange("(o e) -> o e", o=1).broadcast_to([P, E])
                           ).then_inc(gate_b_in, 16)
            nc.gpsimd.affine_select(out=ident[:, :], in_=ident[:, :], compare_op=ALU.not_equal, fill=1.0, base=0,
                                    pattern=[[-1, P]], channel_multiplier=1).then_inc(pool_ready, 1)
            nc.gpsimd.affine_select(out=mask[:, :], in_=mask[:, :], compare_op=ALU.is_ge, fill=MASKED, base=0,
                                    pattern=[[-1, P]], channel_multiplier=1).then_inc(pool_ready, 1)

            with pool.Fori(0, NB) as b:
                for q in range(NQ):
                    pool.wait_ge(x1_stats, b * NQ + q + 1)
                    nc.gpsimd.tensor_copy(bn[:, bass.ds((b * NQ + q) * TPB, TPB), :], bn_now[:, q % 2, :, :])
                    nc.gpsimd.tensor_copy(x_sb[:, bass.ds((b * NQ + q) * BLOCK, BLOCK)], x1[:, q % 2, :]).then_inc(x1_kept, 1)

            with pool.Fori(1, SLOTS) as s:
                with pool.Fori(0, NQ) as half:
                    for par in range(2):
                        u = s * NBLK + half * 2 + par
                        at = bass.ds(half * (2 * BLOCK) + par * BLOCK, BLOCK)
                        pool.wait_ge(yw_ready, START + u + 1)
                        pool.wait_ge(acc_done, START + u - NBLK)
                        nc.gpsimd.tensor_tensor(acc[:, at], acc[:, at], yw[:, par, :], ALU.add).then_inc(acc_done, 1)

        @block.tensor
        def _(pe):
            def transpose4(dst, src, n=TPB):
                for t in range(n):
                    last = nc.tensor.transpose(dst[:, t * P:(t + 1) * P], src[:, t * P:(t + 1) * P], ident[:, :])
                return last

            def three(dst, w_hi, w_lo, m_hi, m_lo, start, stop):
                nc.tensor.matmul(dst, w_hi, m_hi, start=start, stop=False)
                nc.tensor.matmul(dst, w_hi, m_lo, start=False, stop=False)
                return nc.tensor.matmul(dst, w_lo, m_hi, start=False, stop=stop)

            def weights_T(s, loads):
                pe.wait_ge(raw_in[s % 2], 32 * loads)
                for j, src in ((0, raw_up), (1, raw_down)):
                    transpose4(bank[6 + j], src[:, s % 2, :], FC).then_inc(wT_done, 1)

            pe.wait_ge(pool_ready, 6)
            pe.wait_ge(rows_in, 16 * 6)
            nc.tensor.transpose(bank[0][:, 0:P], rows[:, :], ident[:, :]).then_inc(rows_T, 1)
            pe.wait_ge(silu_ready, 1)
            pe.wait_ge(wmod_in, 16)
            for j in range(6):
                last = nc.tensor.matmul(bank[1][:, j * NB:(j + 1) * NB], wmod_sb[:, j * P:(j + 1) * P],
                                        silu[:, 3, :], start=True, stop=True)
            last.then_inc(mod_mm, 1)
            for s in range(2):
                if s:
                    pe.wait_ge(w_lo_done, 2)
                weights_T(s, 1)
            pe.wait_ge(w_lo_done, 4)
            pe.wait_ge(consts_r, 3)

            with pe.Fori(0, NB) as b:
                def wait_turn(item):
                    n = TURN[item]
                    if n < 2:
                        pe.wait_ge(x1_done, START + b * NQ)
                    else:
                        kind, i, k = turn[n - 2]
                        if kind == "x":
                            pe.wait_ge(h_hi_done, b * NQ + i + 1)
                        elif kind == "o":
                            pe.wait_ge(x1_done, START + b * NQ + i + 1)
                        else:
                            g = CHUNK[i] + k
                            pe.wait_ge(pT_dve if g % 2 else pT_act, b * (NCH // 2) + g // 2 + 1)
                    return bank[RING + n % 2]

                def wait_ring(n):
                    m = n - RING
                    if 0 <= m < NPROJ and m % 3 < 2:
                        pe.wait_ge(qk_lo_done, b * (2 * NQ) + m // 3 * 2 + m % 3 + 1)
                    elif 0 <= m < NPROJ:
                        pe.wait_ge(v_done, b * NQ + m // 3 + 1)
                    elif m >= NPROJ:
                        pe.wait_ge(exp_done, b * NCH + m - NPROJ + 1)
                    return bank[n % RING]

                def x_T(q):
                    pe.wait_ge(xn_ready, b * NQ + q + 1)
                    transpose4(wait_turn(("x", q, 0)), xn[:, q % 2, :]).then_inc(xT_done, 1)

                def project(q):
                    pe.wait_ge(h_lo_done, b * NQ + q + 1)
                    for j in range(2):
                        w = slice(j * P, (j + 1) * P)
                        three(wait_ring(3 * q + j)[:, :], wqkv_hi[:, w], wqkv_lo[:, w], hT_hi[:, q % 2, :],
                              hT_lo[:, q % 2, :], True, True).then_inc(proj_done, 1)
                    w = slice(2 * P, 3 * P)
                    dst = wait_ring(3 * q + 2)
                    for t in range(TPB):
                        ts = slice(t * P, (t + 1) * P)
                        last = three(dst[:, ts], hT_hi[:, q % 2, ts], hT_lo[:, q % 2, ts], wqkv_hi[:, w],
                                     wqkv_lo[:, w], True, True)
                    last.then_inc(proj_done, 1)

                def scores(i):
                    if i % TPB == 0:
                        pe.wait_ge(qk_lo_done, b * (2 * NQ) + 2 * (i // TPB) + 2)
                    q_at = slice(i * P, (i + 1) * P)
                    for k in chunks(i):
                        n = key_tiles(i, k) * P
                        dst = wait_ring(NPROJ + CHUNK[i] + k)
                        k_at = slice(SEQ + k * BLOCK, SEQ + k * BLOCK + n)
                        nc.tensor.matmul(dst[:, 0:n], qk_hi[:, q_at], qk_hi[:, k_at], start=True, stop=False)
                        if k == i // TPB:
                            nc.tensor.matmul(dst[:, n - P:n], ident_r[:, :], mask_r[:, :], start=False, stop=False)
                        nc.tensor.matmul(dst[:, 0:n], qk_hi[:, q_at], qk_lo[:, k_at], start=False, stop=False)
                        nc.tensor.matmul(dst[:, 0:n], qk_lo[:, q_at], qk_hi[:, k_at], start=False,
                                         stop=True).then_inc(score_done, 1)

                def probs_T(i):
                    for k in chunks(i):
                        dst = wait_turn(("p", i, k))
                        pe.wait_ge(exp_done, b * NCH + CHUNK[i] + k + 1)
                        transpose4(dst, probs[:, i % 2, k * BLOCK:], key_tiles(i, k)).then_inc(pT_done, 1)

                def pv(q):
                    pe.wait_ge(v_done, b * NQ + q + 1)
                    pe.wait_ge(oT_ready, START + b * NQ + q)
                    done = CHUNK[TPB * (q + 1)]
                    pe.wait_ge(pT_act, b * (NCH // 2) + (done + 1) // 2)
                    pe.wait_ge(pT_dve, b * (NCH // 2) + done // 2)
                    last = TPB * (q + 1) - 1
                    for j in range(last + 1):
                        lo = max(0, j - TPB * q) * P
                        mm = nc.tensor.matmul(bank[7][:, lo:BLOCK], v_sb[:, j * P:(j + 1) * P],
                                              probsT[:, j * BLOCK + lo:(j + 1) * BLOCK], start=(j == 0),
                                              stop=(j == last))
                    mm.then_inc(pv_done, 1)

                def o_T(q):
                    dst = wait_turn(("o", q, 0))
                    pe.wait_ge(oT_ready, START + b * NQ + q + 1)
                    transpose4(dst, oT[:, q % 2, :]).then_inc(oTT_done, 1)

                x_T(0)
                for q in range(NQ):
                    if q + 1 < NQ:
                        x_T(q + 1)
                    project(q)
                for i in range(NT + 1):
                    if i < NT:
                        scores(i)
                    if i % TPB == 1 and i > 1:
                        o_T(i // TPB - 1)
                    if i > 0:
                        probs_T(i - 1)
                    if i % TPB == 0 and i > 0:
                        pv(i // TPB - 1)
                o_T(NQ - 1)

            pe.wait_ge(x1_done, START + NBLK)
            def x2_T(n):
                pe.wait_ge(x2n_ready, n + 1)
                if n >= 2:
                    pe.wait_ge(h2_hi_done, n - 1)
                transpose4(bank[5 + n % 2], xn[:, n % 2, :]).then_inc(x2T_done, 1)

            def gate(n):
                pe.wait_ge(h2_hi_done, n + 1)
                for t in range(TPB):
                    at = (n * TPB + t) * E
                    last = nc.tensor.matmul(bank[7][:, at:at + E], hT[:, n % 2, t * P:(t + 1) * P],
                                            cols[:, ROW_GATE:ROW_GATE + E], start=True, stop=True)
                last.then_inc(gate_done, 1)

            x2_T(0)
            for n in range(NBLK):
                if n + 1 < NBLK:
                    x2_T(n + 1)
                gate(n)
            pe.wait_ge(h2_lo_done, NBLK)

            def up(s, u, blk, at):
                for f in range(FC):
                    fs = slice(f * P, (f + 1) * P)
                    if not (isinstance(u, int) and u < 1):
                        pe.wait_ge(gelu_done, FC * u - FC + f + 1)
                    three(bank[f][:, :], up_hi[:, s % 2, fs], up_lo[:, s % 2, fs], h2_hi[:, bass.ds(at, BLOCK)],
                          h2_lo[:, bass.ds(at, BLOCK)], True, True).then_inc(up_done, 1)

            def down(s, u, par):
                if not (isinstance(u, int) and u < 2):
                    pe.wait_ge(yw_ready, START + u - 1)
                for f in range(FC):
                    if f % 2 == 0:
                        pe.wait_ge(a_lo_done, 2 * u + f // 2 + 1)
                    fs, at = slice(f * P, (f + 1) * P), slice(f * BLOCK, (f + 1) * BLOCK)
                    mm = three(bank[4 + par][:, :], down_hi[:, s % 2, fs], down_lo[:, s % 2, fs],
                               a_hi[:, par, at], a_lo[:, par, at], f == 0, f == FC - 1)
                mm.then_inc(down_done, 1)

            def slot(s, base, n_slot, loads, prefetch):
                pe.wait_ge(w_lo_done, 2 * n_slot + 2)
                up(s, base, 0, 0)
                if not (isinstance(base, int) and base == 0):
                    down(s + 1, base - 1, 1)
                up(s, base + 1, 1, BLOCK)
                down(s, base, 0)
                if prefetch:
                    weights_T(s + 1, loads)
                with pe.Fori(1, NBLK // 2) as it:
                    up(s, base + it * 2, 0, it * (2 * BLOCK))
                    down(s, base + it * 2 - 1, 1)
                    up(s, base + it * 2 + 1, 1, it * (2 * BLOCK) + BLOCK)
                    down(s, base + it * 2, 0)

            slot(0, 0, 0, 0, False)
            pe.wait_ge(weight_ready, 1)
            for b in range(NB):
                last = nc.tensor.transpose(bank[6][:, b * P:(b + 1) * P], weight[:, b * NT * E:(b + 1) * NT * E], ident[:, :])
            last.then_inc(weightT_mm, 1)
            pe.wait_ge(weightT_ready, NB)
            with pe.Fori(0, (SLOTS - 3) // 2) as pair:
                for par in (1, 2):
                    n = pair * 2 + par
                    slot(par, n * NBLK, n, pair + 2, True)
            slot(SLOTS - 2, (SLOTS - 2) * NBLK, SLOTS - 2, (SLOTS - 1) // 2 + 1, True)
            slot(SLOTS - 1, (SLOTS - 1) * NBLK, SLOTS - 1, 0, False)
            down(SLOTS - 1, SLOTS * NBLK - 1, 1)

            pe.wait_ge(gelu_done, SLOTS * NBLK * FC)
            for n in range(NBLK):
                pe.wait_ge(accg_ready, n + 1)
                if n >= 2:
                    pe.wait_ge(out_ready, n - 1)
                transpose4(bank[n % 2], oT[:, n % 2, :]).then_inc(accT_done, 1)

        @block.scalar
        def _(act):
            act.sem_inc(oT_ready, START)

            def weights_hi(s, n_slot):
                for j, dst in ((0, up_hi), (1, down_hi)):
                    act.wait_ge(wT_done, 2 * n_slot + j + 1)
                    nc.scalar.copy(dst[:, s % 2, :], bank[6 + j][:, :]).then_inc(w_hi_done, 1)

            act.wait_ge(cols_ready, 1)
            nc.scalar.activation(silu[:, 0, :], cols[:, ROW_C:ROW_C + NB], ACT.Exp, scale=-1.0).then_inc(silu_exp, 1)
            weights_hi(0, 0)
            weights_hi(1, 1)
            act.wait_ge(var_ready, 1)
            nc.scalar.activation(std[:, :], var[:, :], ACT.Sqrt).then_inc(std_ready, 1)
            act.wait_ge(mods_ready, 1)

            with act.Fori(0, NB) as b:
                def h_hi(q):
                    act.wait_ge(xT_done, b * NQ + q + 1)
                    if q >= 2:
                        act.wait_ge(h_lo_done, b * NQ + q - 1)
                        act.wait_ge(proj_done, b * NPROJ + 3 * (q - 1))
                    src = bank[RING + TURN[("x", q, 0)] % 2]
                    nc.scalar.activation(hT[:, q % 2, :], src[:, :], ACT.Identity, bias=mod_now[:, SA:SA + 1], scale=mod_now[:, CA:CA + 1])
                    nc.scalar.activation(hT_hi[:, q % 2, :], src[:, :], ACT.Identity, bias=mod_now[:, SA:SA + 1],
                                         scale=mod_now[:, CA:CA + 1]).then_inc(h_hi_done, 1)

                def qkv(q):
                    for j in range(2):
                        act.wait_ge(proj_done, b * NPROJ + 3 * q + j + 1)
                        nc.scalar.copy(qk_hi[:, j * SEQ + q * BLOCK:j * SEQ + (q + 1) * BLOCK],
                                       bank[(3 * q + j) % RING][:, :]).then_inc(qk_hi_done, 1)
                    act.wait_ge(proj_done, b * NPROJ + 3 * q + 3)
                    nc.scalar.copy(v_sb[:, q * BLOCK:(q + 1) * BLOCK],
                                   bank[(3 * q + 2) % RING][:, :]).then_inc(v_done, 1)

                def exps(i, k):
                    if k == 0:
                        act.wait_ge(neg_max_ready, b * NT + i + 1)
                        if i >= 2:
                            act.wait_ge(pT_done, b * NCH + CHUNK[i - 1])
                    n = key_tiles(i, k) * P
                    nc.scalar.activation(probs[:, i % 2, k * BLOCK:k * BLOCK + n],
                                         bank[(NPROJ + CHUNK[i] + k) % RING][:, 0:n], ACT.Exp,
                                         bias=neg_max[:, i:i + 1], scale=SCALE,
                                         accum_out=exp_sum[:, i, k:k + 1]).then_inc(exp_done, 1)

                def probs_out(i, k):
                    if (CHUNK[i] + k) % 2 == 0:
                        act.wait_ge(pT_done, b * NCH + CHUNK[i] + k + 1)
                        if i // TPB > 0:
                            act.wait_ge(pv_done, b * NQ + i // TPB)
                        n = key_tiles(i, k)
                        at = i % TPB * P
                        dst = probsT[:, :].rearrange("p (j t) -> p j t", t=BLOCK)
                        src = bank[RING + TURN[("p", i, k)] % 2][:, 0:n * P].rearrange("p (j t) -> p j t", t=P)
                        nc.scalar.copy(dst[:, TPB * k:TPB * k + n, at:at + P], src).then_inc(pT_act, 1)

                def o_out(q):
                    act.wait_ge(pv_done, b * NQ + q + 1)
                    if q >= 2:
                        act.wait_ge(oTT_done, b * NQ + q - 1)
                    nc.scalar.activation(oT[:, q % 2, :], bank[7][:, :], ACT.Copy,
                                         scale=mod_now[:, GA:GA + 1]).then_inc(oT_ready, 1)

                h_hi(0)
                for q in range(NQ):
                    if q + 1 < NQ:
                        h_hi(q + 1)
                    qkv(q)
                for i in range(NT + 1):
                    if i % TPB == 1 and i > 1:
                        o_out(i // TPB - 1)
                    for k in range(NQ):
                        if i < NT and k in chunks(i):
                            exps(i, k)
                        if i > 0 and k in chunks(i - 1):
                            probs_out(i - 1, k)
                o_out(NQ - 1)

            act.wait_ge(var_ready, 2)
            nc.scalar.activation(std[:, :], var[:, :], ACT.Sqrt).then_inc(std_ready, 1)
            for n in range(NBLK):
                act.wait_ge(x2T_done, n + 1)
                if n >= 2:
                    act.wait_ge(gate_done, n - 1)
                    act.wait_ge(h2_lo_done, n - 1)
                at, b, src = slice(n * BLOCK, (n + 1) * BLOCK), n // NQ, bank[5 + n % 2][:, :]
                nc.scalar.activation(hT[:, n % 2, :], src, ACT.Identity, bias=mod(SB, b), scale=mod(CB, b))
                nc.scalar.activation(h2_hi[:, at], src, ACT.Identity, bias=mod(SB, b),
                                     scale=mod(CB, b)).then_inc(h2_hi_done, 1)

            act.wait_ge(logit_ready, 1)
            nc.scalar.activation(score[:, :, :].rearrange("p n e -> p (n e)"), logits[:, :], ACT.Exp,
                                 scale=-1.0).then_inc(sig_exp, 1)

            def gelus(s, u, par):
                for f in range(FC):
                    act.wait_ge(up_done, FC * u + f + 1)
                    if f % 2 == 0 and not (isinstance(u, int) and u < 2):
                        act.wait_ge(a_lo_done, 2 * u + f // 2 - 3)
                    nc.scalar.activation(a_sb[:, par, f * BLOCK:(f + 1) * BLOCK], bank[f][:, :], ACT.Gelu,
                                         bias=bias_now[:, s % 2, f:f + 1]).then_inc(gelu_done, 1)

            def slot(s, base, n_slot, prefetch):
                act.wait_ge(w_lo_done, 2 * n_slot + 2)
                gelus(s, base, 0)
                gelus(s, base + 1, 1)
                if prefetch:
                    act.wait_ge(down_done, base)
                    weights_hi(s + 1, n_slot + 1)
                with act.Fori(1, NBLK // 2) as it:
                    for par in range(2):
                        gelus(s, base + it * 2 + par, par)

            slot(0, 0, 0, False)
            with act.Fori(0, (SLOTS - 3) // 2) as pair:
                for par in (1, 2):
                    slot(par, (pair * 2 + par) * NBLK, pair * 2 + par, True)
            slot(SLOTS - 2, (SLOTS - 2) * NBLK, SLOTS - 2, True)
            slot(SLOTS - 1, (SLOTS - 1) * NBLK, SLOTS - 1, False)

            for n in range(NBLK):
                act.wait_ge(acc_done, START + (SLOTS - 2) * NBLK + n + 1)
                if n >= 2:
                    act.wait_ge(accT_done, n - 1)
                nc.scalar.activation(oT[:, n % 2, :], acc[:, n * BLOCK:(n + 1) * BLOCK], ACT.Copy,
                                     scale=mod(GB, n // NQ)).then_inc(accg_ready, 1)

        @block.vector
        def _(dve):
            dve.sem_inc(x1_done, START)
            dve.sem_inc(yw_ready, START)

            def weights_lo(s, n_slot):
                nc.vector.tensor_copy(bias_now[:, s % 2, :], cols[:, bass.ds(n_slot * FC + ROW_BU, FC)])
                for j, hi, lo in ((0, up_hi, up_lo), (1, down_hi, down_lo)):
                    dve.wait_ge(w_hi_done, 2 * n_slot + j + 1)
                    nc.vector.tensor_tensor(lo[:, s % 2, :], bank[6 + j][:, :], hi[:, s % 2, :].bitcast(F32),
                                            ALU.subtract).then_inc(w_lo_done, 1)

            step = Steps()

            dve.wait_ge(pool_ready, 6)
            nc.vector.tensor_copy(ident_r[:, :], ident[:, :]).then_inc(consts_r, 1)
            nc.vector.tensor_copy(mask_r[:, :], mask[:, :])
            dve.wait_ge(rows_T, 1)
            nc.vector.tensor_copy(cols[:, :], bank[0][:, 0:ROWS]).then_inc(cols_ready, 1)
            dve.wait_ge(qkv_in, 48)
            nc.vector.tensor_copy(wqkv_hi[:, :], wqkv[:, :]).then_inc(consts_r, 1)
            dve.wait_ge(consts_r, 2)
            nc.vector.tensor_tensor(wqkv_lo[:, :], wqkv[:, :], wqkv_hi[:, :].bitcast(F32), ALU.subtract).then_inc(consts_r, 1)

            dve.wait_ge(silu_exp, 1)
            nc.vector.tensor_scalar(silu[:, 1, :], silu[:, 0, :], 1.0, None, ALU.add).then_inc(dve_step, 1)
            dve.wait_ge(dve_step, step.next())
            nc.vector.reciprocal(silu[:, 2, :], silu[:, 1, :]).then_inc(dve_step, 1)
            dve.wait_ge(dve_step, step.next())
            dve.wait_ge(cols_ready, 1)
            nc.vector.tensor_tensor(silu[:, 3, :], silu[:, 2, :], cols[:, ROW_C:ROW_C + NB], ALU.mult).then_inc(silu_ready, 1)

            weights_lo(0, 0)
            weights_lo(1, 1)

            dve.wait_ge(mod_mm, 1)
            for j in (SA, SB):
                nc.vector.tensor_copy(mods[:, j * NB:(j + 1) * NB], bank[1][:, j * NB:(j + 1) * NB])
            for j in (CA, CB):
                nc.vector.tensor_scalar(mods[:, j * NB:(j + 1) * NB], bank[1][:, j * NB:(j + 1) * NB], 1.0, None, ALU.add)
            for j in (GA, GB):
                at = slice(j * NB, (j + 1) * NB)
                nc.vector.tensor_scalar(gsign[:, :], bank[1][:, at], 0.0, 2.0, ALU.is_ge, ALU.mult).then_inc(dve_step, 1)
                dve.wait_ge(dve_step, step.next())
                nc.vector.tensor_scalar(gsign[:, :], gsign[:, :], -1.0, None, ALU.add).then_inc(dve_step, 1)
                dve.wait_ge(dve_step, step.next())
                nc.vector.tensor_tensor(mods[:, at], gsign[:, :], bank[1][:, at], ALU.mult).then_inc(dve_step, 1)
                dve.wait_ge(dve_step, step.next())
                nc.vector.scalar_tensor_tensor(out=mods[:, at], in0=mods[:, at], scalar=0.25, in1=gsign[:, :],
                                               op0=ALU.max, op1=ALU.mult).then_inc(dve_step, 1)
                dve.wait_ge(dve_step, step.next())
            nc.vector.memset(newton[:, :], 0.0).then_inc(mods_ready, 1)

            for n in range(TILES):
                if n % (NT // 2) == 0:
                    dve.wait_ge(x_in[n // (NT // 2)], 16)
                last = nc.vector.bn_stats(bn[:, n, :], x_sb[:, n * P:(n + 1) * P])
            last.then_inc(dve_step, 1)
            dve.wait_ge(dve_step, step.next())

            def variance():
                nc.vector.tensor_tensor(mean[:, :], bn[:, :, 1], bn[:, :, 4], ALU.add)
                nc.vector.tensor_tensor(std[:, :], bn[:, :, 1], bn[:, :, 4], ALU.subtract)
                nc.vector.tensor_tensor(var[:, :], bn[:, :, 2], bn[:, :, 5], ALU.add).then_inc(dve_step, 1)
                dve.wait_ge(dve_step, step.next())
                nc.vector.tensor_scalar(mean[:, :], mean[:, :], 0.5, None, ALU.mult)
                nc.vector.tensor_tensor(newton[:, :], std[:, :], std[:, :], ALU.mult)
                nc.vector.tensor_scalar(var[:, :], var[:, :], 1.0 / P, LN_EPS, ALU.mult, ALU.add).then_inc(dve_step, 1)
                dve.wait_ge(dve_step, step.next())
                nc.vector.scalar_tensor_tensor(out=var[:, :], in0=newton[:, :], scalar=0.25, in1=var[:, :],
                                               op0=ALU.mult, op1=ALU.add).then_inc(var_ready, 1)

            def inverse_std(nth):
                dve.wait_ge(std_ready, nth)
                nc.vector.reciprocal(std[:, :], std[:, :]).then_inc(dve_step, 1)
                dve.wait_ge(dve_step, step.next())
                nc.vector.tensor_tensor(newton[:, :], std[:, :], std[:, :], ALU.mult).then_inc(dve_step, 1)
                dve.wait_ge(dve_step, step.next())
                nc.vector.tensor_tensor(newton[:, :], newton[:, :], var[:, :], ALU.mult).then_inc(dve_step, 1)
                dve.wait_ge(dve_step, step.next())
                nc.vector.tensor_scalar(newton[:, :], newton[:, :], -0.5, 1.5, ALU.mult, ALU.add).then_inc(dve_step, 1)
                dve.wait_ge(dve_step, step.next())
                nc.vector.tensor_tensor(rstd[:, :], newton[:, :], std[:, :], ALU.mult).then_inc(dve_step, 1)
                dve.wait_ge(dve_step, step.next())

            def normalise(dst, tile, t):
                return nc.vector.tensor_scalar(dst[:, t * P:(t + 1) * P], x_sb[:, tok(tile)],
                                               mean[:, bass.ds(tile, 1)], rstd[:, bass.ds(tile, 1)],
                                               ALU.subtract, ALU.mult)

            variance()
            inverse_std(1)

            STEPS = NT + 2 * NQ
            before = step.n
            with dve.Fori(0, NB) as b:
                own = Steps(b * STEPS + before)

                def x_norm(q):
                    if q >= 2:
                        dve.wait_ge(xT_done, b * NQ + q - 1)
                    for t in range(TPB):
                        last = normalise(xn[:, q % 2, :], b * NT + q * TPB + t, t)
                    last.then_inc(xn_ready, 1)

                def h_low(q):
                    dve.wait_ge(h_hi_done, b * NQ + q + 1)
                    if q >= 2:
                        dve.wait_ge(proj_done, b * NPROJ + 3 * (q - 1))
                    nc.vector.tensor_tensor(hT_lo[:, q % 2, :], hT[:, q % 2, :], hT_hi[:, q % 2, :].bitcast(F32),
                                            ALU.subtract).then_inc(h_lo_done, 1)

                def qk_low(q):
                    for j in range(2):
                        at = slice(j * SEQ + q * BLOCK, j * SEQ + (q + 1) * BLOCK)
                        dve.wait_ge(qk_hi_done, b * (2 * NQ) + 2 * q + j + 1)
                        nc.vector.tensor_tensor(qk_lo[:, at], bank[(3 * q + j) % RING][:, :],
                                                qk_hi[:, at].bitcast(F32), ALU.subtract).then_inc(qk_lo_done, 1)

                def row_max(i):
                    for k in chunks(i):
                        n = key_tiles(i, k) * P
                        dve.wait_ge(score_done, b * NCH + CHUNK[i] + k + 1)
                        last = nc.vector.tensor_reduce(chunk_max[:, i % 2, k:k + 1],
                                                       bank[(NPROJ + CHUNK[i] + k) % RING][:, 0:n], AX_X, ALU.max)
                    last.then_inc(dve_step, 1)
                    dve.wait_ge(dve_step, own.next())
                    n = i // TPB + 1
                    nc.vector.tensor_scalar(max_junk[:, i % 2, 0:n], chunk_max[:, i % 2, 0:n], -SCALE, None, ALU.mult,
                                            ALU.min, accum_out=neg_max[:, i:i + 1]).then_inc(neg_max_ready, 1)

                def probs_out(i, k):
                    if (CHUNK[i] + k) % 2:
                        dve.wait_ge(pT_done, b * NCH + CHUNK[i] + k + 1)
                        if i // TPB > 0:
                            dve.wait_ge(pv_done, b * NQ + i // TPB)
                        n = key_tiles(i, k)
                        at = i % TPB * P
                        dst = probsT[:, :].rearrange("p (j t) -> p j t", t=BLOCK)
                        src = bank[RING + TURN[("p", i, k)] % 2][:, 0:n * P].rearrange("p (j t) -> p j t", t=P)
                        nc.vector.tensor_copy(dst[:, TPB * k:TPB * k + n, at:at + P], src).then_inc(pT_dve, 1)

                def residual(q):
                    dve.wait_ge(exp_done, b * NCH + CHUNK[TPB * (q + 1)])
                    nc.vector.reduce_sum(row_sum[:, :], exp_sum[:, TPB * q:TPB * (q + 1), 0:q + 1], AX_X).then_inc(dve_step, 1)
                    dve.wait_ge(dve_step, own.next())
                    nc.vector.reciprocal(row_inv[:, :], row_sum[:, :]).then_inc(dve_step, 1)
                    dve.wait_ge(dve_step, own.next())
                    dve.wait_ge(oTT_done, b * NQ + q + 1)
                    src = bank[RING + TURN[("o", q, 0)] % 2]
                    if q >= 2:
                        dve.wait_ge(x1_kept, START + b * NQ + q - 1)
                    for t in range(TPB):
                        ts = slice(t * P, (t + 1) * P)
                        last = nc.vector.scalar_tensor_tensor(out=x1[:, q % 2, ts], in0=src[:, ts],
                                                              scalar=row_inv[:, t:t + 1],
                                                              in1=x_sb[:, tok(b * NT + q * TPB + t)],
                                                              op0=ALU.mult, op1=ALU.add)
                    last.then_inc(x1_done, 1)
                    dve.wait_ge(x1_done, START + b * NQ + q + 1)
                    for t in range(TPB):
                        last = nc.vector.bn_stats(bn_now[:, q % 2, t, :], x1[:, q % 2, t * P:(t + 1) * P])
                    last.then_inc(x1_stats, 1)

                dve.wait_ge(x1_kept, START + b * NQ)
                nc.vector.tensor_copy(mod_now[:, :], mods[:, :].rearrange("p (j b) -> p b j", b=NB)[:, bass.ds(b, 1), :]
                                      .rearrange("p o j -> p (o j)"))
                x_norm(0)
                x_norm(1)
                h_low(0)
                for q in range(NQ):
                    if q + 2 < NQ:
                        x_norm(q + 2)
                    if q + 1 < NQ:
                        h_low(q + 1)
                    qk_low(q)
                for i in range(NT + 1):
                    if i < NT:
                        row_max(i)
                    if i % TPB == 1 and i > 1:
                        residual(i // TPB - 1)
                    if i > 0:
                        for k in chunks(i - 1):
                            probs_out(i - 1, k)
                residual(NQ - 1)
                assert own.n == STEPS
            step.n = before + NB * STEPS

            dve.wait_ge(x1_kept, START + NBLK)
            variance()
            inverse_std(2)
            def x2_norm(n):
                if n >= 2:
                    dve.wait_ge(x2T_done, n - 1)
                for t in range(TPB):
                    last = normalise(xn[:, n % 2, :], n * TPB + t, t)
                last.then_inc(x2n_ready, 1)

            def h2_low(n):
                at = slice(n * BLOCK, (n + 1) * BLOCK)
                dve.wait_ge(h2_hi_done, n + 1)
                nc.vector.tensor_tensor(h2_lo[:, at], hT[:, n % 2, :], h2_hi[:, at].bitcast(F32),
                                        ALU.subtract).then_inc(h2_lo_done, 1)

            x2_norm(0)
            for n in range(NBLK):
                if n + 1 < NBLK:
                    x2_norm(n + 1)
                h2_low(n)
            dve.wait_ge(gate_b_in, 16)
            dve.wait_ge(gate_done, NBLK)
            nc.vector.tensor_tensor(logits[:, :].rearrange("p (n e) -> p n e", e=E),
                                    bank[7][:, 0:TILES * E].rearrange("p (n e) -> p n e", e=E),
                                    gate_b[:, :].rearrange("p (o e) -> p o e", o=1).broadcast_to([P, TILES, E]),
                                    ALU.add).then_inc(logit_ready, 1)

            def per_expert(ap):
                return ap.rearrange("p (n o) -> p n o", o=1).broadcast_to([P, TILES, E])

            count = down_count[:, :].rearrange("p (o e) -> p o e", o=1).broadcast_to([P, TILES, E])
            dve.wait_ge(sig_exp, 1)
            nc.vector.tensor_scalar(score[:, :, :], score[:, :, :], 1.0, None, ALU.add).then_inc(dve_step, 1)
            dve.wait_ge(dve_step, step.next())
            nc.vector.reciprocal(score[:, :, :], score[:, :, :]).then_inc(dve_step, 1)
            dve.wait_ge(dve_step, step.next())
            for n, pick in enumerate((pick1, pick2)):
                top, who = best[:, n, :], best[:, 2, :]
                nc.vector.tensor_reduce(top, score[:, :, :], AX_X, ALU.max).then_inc(dve_step, 1)
                dve.wait_ge(dve_step, step.next())
                nc.vector.tensor_tensor(tie[:, :, :], score[:, :, :], per_expert(top), ALU.is_equal).then_inc(dve_step, 1)
                dve.wait_ge(dve_step, step.next())
                nc.vector.tensor_tensor(tie[:, :, :], tie[:, :, :], count, ALU.mult).then_inc(dve_step, 1)
                dve.wait_ge(dve_step, step.next())
                nc.vector.tensor_reduce(who, tie[:, :, :], AX_X, ALU.max).then_inc(dve_step, 1)
                dve.wait_ge(dve_step, step.next())
                nc.vector.tensor_tensor(pick[:, :, :], tie[:, :, :], per_expert(who), ALU.is_equal).then_inc(dve_step, 1)
                dve.wait_ge(dve_step, step.next())
                if n == 0:
                    nc.vector.scalar_tensor_tensor(out=score[:, :, :], in0=pick[:, :, :], scalar=-4.0,
                                                   in1=score[:, :, :], op0=ALU.mult, op1=ALU.add).then_inc(dve_step, 1)
                    dve.wait_ge(dve_step, step.next())
            nc.vector.tensor_tensor(best[:, 2, :], best[:, 0, :], best[:, 1, :], ALU.add).then_inc(dve_step, 1)
            dve.wait_ge(dve_step, step.next())
            nc.vector.tensor_scalar(best[:, 2, :], best[:, 2, :], 1e-6, None, ALU.add).then_inc(dve_step, 1)
            dve.wait_ge(dve_step, step.next())
            nc.vector.reciprocal(best[:, 3, :], best[:, 2, :]).then_inc(dve_step, 1)
            dve.wait_ge(dve_step, step.next())
            for n, pick in enumerate((pick1, pick2)):
                nc.vector.tensor_tensor(best[:, n, :], best[:, n, :], best[:, 3, :], ALU.mult).then_inc(dve_step, 1)
                dve.wait_ge(dve_step, step.next())
                nc.vector.tensor_tensor(pick[:, :, :], pick[:, :, :], per_expert(best[:, n, :]), ALU.mult).then_inc(dve_step, 1)
                dve.wait_ge(dve_step, step.next())
            nc.vector.tensor_tensor(weight[:, :].rearrange("p (n e) -> p n e", e=E), pick1[:, :, :], pick2[:, :, :],
                                    ALU.add).then_inc(weight_ready, 1)

            def split(u, par):
                for h in range(FC // 2):
                    at = slice(h * 2 * BLOCK, (h + 1) * 2 * BLOCK)
                    dve.wait_ge(gelu_done, FC * u + 2 * h + 2)
                    if h == 0 and not (isinstance(u, int) and u < 2):
                        dve.wait_ge(down_done, u - 1)
                    nc.vector.tensor_copy(a_hi[:, par, at], a_sb[:, par, at]).then_inc(a_hi_done, 1)
                    dve.wait_ge(a_hi_done, 2 * u + h + 1)
                    nc.vector.tensor_tensor(a_lo[:, par, at], a_sb[:, par, at], a_hi[:, par, at].bitcast(F32),
                                            ALU.subtract).then_inc(a_lo_done, 1)

            def weigh(u, par, blk, n_slot, shared):
                dve.wait_ge(down_done, u + 1)
                bias = cols[:, bass.ds(n_slot + ROW_BD, 1)]
                if shared:
                    nc.vector.tensor_scalar(acc[:, bass.ds(blk * BLOCK, BLOCK)], bank[4 + par][:, :], bias, 0.1,
                                            ALU.add, ALU.mult).then_inc(yw_ready, 1)
                else:
                    if not (isinstance(u, int) and u < NBLK + 2):
                        dve.wait_ge(acc_done, START + u - NBLK - 1)
                    w = w_bc[:, :, :].rearrange("p b t -> p (b t)")[:, bass.ds(blk * BLOCK, BLOCK)]
                    nc.vector.scalar_tensor_tensor(out=yw[:, par, :], in0=bank[4 + par][:, :], scalar=bias, in1=w,
                                                   op0=ALU.add, op1=ALU.mult).then_inc(yw_ready, 1)

            def slot(s, base, n_slot, prefetch, first=False, second=False):
                split(base, 0)
                if not first:
                    weigh(base - 1, 1, NBLK - 1, n_slot - 1, second)
                split(base + 1, 1)
                if not first:
                    dve.wait_ge(w_bc_in[0], n_slot * 16)
                weigh(base, 0, 0, n_slot, first)
                if prefetch:
                    weights_lo(s + 1, n_slot + 1)
                with dve.Fori(1, NBLK // 2) as it:
                    split(base + it * 2, 0)
                    weigh(base + it * 2 - 1, 1, it * 2 - 1, n_slot, first)
                    if not first:
                        dve.wait_ge(w_bc_in[1], n_slot * 16)
                    split(base + it * 2 + 1, 1)
                    weigh(base + it * 2, 0, it * 2, n_slot, first)

            slot(0, 0, 0, False, first=True)
            dve.wait_ge(weightT_mm, 1)
            for b in range(NB):
                nc.vector.tensor_copy(weightT[:, b, :], bank[6][:, b * P:(b + 1) * P]).then_inc(weightT_ready, 1)
            slot(1, NBLK, 1, True, second=True)
            with dve.Fori(0, (SLOTS - 3) // 2) as pair:
                for par in (2, 3):
                    slot(par, (pair * 2 + par) * NBLK, pair * 2 + par, True)
            slot(SLOTS - 1, (SLOTS - 1) * NBLK, SLOTS - 1, False)
            weigh(SLOTS * NBLK - 1, 1, NBLK - 1, SLOTS - 1, False)

            for n in range(NBLK):
                dve.wait_ge(accT_done, n + 1)
                at = slice(n * BLOCK, (n + 1) * BLOCK)
                nc.vector.tensor_tensor(x_sb[:, at], bank[n % 2][:, :], x_sb[:, at], ALU.add).then_inc(out_ready, 1)


_INS = ['L0_attn_x', 'L0_attn_Wk', 'L0_attn_Wq', 'L0_attn_Wv', 'L0_ffn_gate_w', 'L0_ffn_gate_bias', 'L0_ffn_Wu',
        'L0_ffn_bu', 'L0_ffn_Wd', 'L0_ffn_bd', 'L0_ffn_sWu', 'L0_ffn_sbu', 'L0_ffn_sWd', 'L0_ffn_sbd', 'L0_c', 'L0_wmod']


def kernel(**inputs):
    import numpy as _np
    import concourse.bacc as _bacc
    from concourse import mybir as _mybir
    from concourse.bass_utils import run_bass_kernel_spmd as _run

    nc = _bacc.Bacc("TRN2", target_bir_lowering=False, num_devices=1)
    arrays, args = {}, []
    for name in _INS:
        a = _np.ascontiguousarray(inputs[name])
        arrays[f"in_{name}_dram"] = a
        args.append(nc.dram_tensor(f"in_{name}_dram", a.shape, _mybir.dt.from_np(a.dtype), kind="ExternalInput").ap())
    shape = inputs["L0_attn_x"].shape
    args.append(nc.dram_tensor("out_0_dram", shape, _mybir.dt.float32, kind="ExternalOutput").ap())
    adaln_attention_moe(nc, *args)
    r = _run(nc, [arrays], core_ids=[0])
    return r.results[0]["out_0_dram"]
```

```python
from contextlib import ExitStack

import concourse.bass as bass
from concourse import mybir

ALU = mybir.AluOpType
ACT = mybir.ActivationFunctionType
F32 = mybir.dt.float32
F32R = mybir.dt.float32r
AX_X = mybir.AxisListType.X

P = 128
BLOCK = 512
TPB = BLOCK // P
MASKED = -1.0e30
LN_EPS = 1e-5



PROJECT_AHEAD = 5


def pair_order(batches, pairs):
    return [(b, p) for b in range(batches) for p in range(pairs)]


class Steps:

    def __init__(self, base=0):
        self.base, self.n = base, 0

    def next(self):
        self.n += 1
        return self.base + self.n


def adaln_attention_moe(nc, x, Wk, Wq, Wv, gate_w, gate_bias, Wu, bu, Wd, bd, sWu, sbu, sWd, sbd, c, wmod, out):
    NB, SEQ, D = x.shape
    E, F, _ = Wu.shape
    assert D == P and SEQ % BLOCK == 0 and F % P == 0
    NT = SEQ // P
    NQ = SEQ // BLOCK
    TILES = NB * NT
    FC = F // P
    SLOTS = E + 1
    NBLK = NB * NQ
    SUM_LAG = 3
    SCALE = float(D) ** -0.5

    NPAIR = NT // 2
    PAIR = 2 * P
    ORDER = pair_order(NB, NPAIR)
    TILE = [(b, 2 * p + t) for b, p in ORDER for t in range(2)]
    NTILE = len(TILE)
    assert NTILE == TILES

    def chunks(i):
        return range(TILE[i][1] // TPB + 1)

    def key_tiles(i, k):
        t = TILE[i][1]
        return TPB if k < t // TPB else t % TPB + 1

    CHUNK = [0]
    for i in range(NTILE):
        CHUNK.append(CHUNK[-1] + len(chunks(i)))
    NCH = CHUNK[NTILE]

    TURN_LAG = 1
    EXP_LEAD = 1

    def turned_in(i):
        return i - TURN_LAG if 0 <= i - TURN_LAG < NTILE else None

    def pv_of(i):
        n = i - 2 - TURN_LAG
        return (n // 2, n % 2) if 0 <= n < NTILE else None

    def added_at(r):
        return 2 * r + 4 + TURN_LAG

    def added_in(i):
        n = i - 4 - TURN_LAG
        return n // 2 if n % 2 == 0 and 0 <= n < NTILE else None

    FIRST = [(TILE.index((b, q * TPB)), b, q) for b in range(NB) for q in range(NQ)]
    BLOCKS = [(b, q) for _, b, q in sorted(FIRST)]
    STARTS = []
    for first, b, q in sorted(FIRST, reverse=True):
        STARTS.insert(0, min([first - PROJECT_AHEAD] + [n - 2 for n in STARTS[:1]]))
    STARTS[1] = min(STARTS[1], STARTS[0] + 2)
    NUMBER = {block: n for n, block in enumerate(BLOCKS)}
    LAST_TILE = [TILE.index((b, q * TPB + TPB - 1)) for b, q in BLOCKS]
    QRING = 3
    assert all(LAST_TILE[n - QRING] < STARTS[n] + 1 + QK for n in range(QRING, len(BLOCKS)) for QK in (1,))

    def phase(i, lag):
        return STARTS.index(i - lag) if i - lag in STARTS else None

    FINISH = [(added_at(ORDER.index((b, 2 * q + 1))), b, q) for b in range(NB) for q in range(NQ)]
    DONE = [(b, q) for _, b, q in sorted(FINISH)]
    DONE_AT = [at for at, _, _ in sorted(FINISH)]

    def second(i, lag):
        return DONE_AT.index(i - lag) if i - lag in DONE_AT else None

    FIRST_STEP = STARTS[0] - 3
    STEPS = DONE_AT[-1] + 5
    X_STATS, X_NORM, X_T, X_QK, X_V = -3, -1, 0, 1, 2
    Y_STATS, Y_NORM, Y_T, Y_GATE = 0, 2, 3, 4

    def weights_in(i):
        return {STARTS[0] - 1: 0, WEIGHTS_1: 1}.get(i)

    WEIGHTS_1 = 3
    assert WEIGHTS_1 < STARTS[BLOCKS.index((1, 0))] + X_V

    SHARED_AT = [NTILE + TURN_LAG, DONE_AT[-1], DONE_AT[-1] + Y_NORM, DONE_AT[-1] + Y_T]
    assert DONE == [(b, q) for b in range(NB) for q in range(NQ)]
    Y_BANK = (4, 7)

    RING, TURNS = 4, 3
    ring = []
    for i in range(FIRST_STEP, STEPS):
        if phase(i, X_QK) is not None:
            ring += [("q", phase(i, X_QK), 0), ("k", phase(i, X_QK), 0)]
        if phase(i, X_V) is not None:
            ring += [("v", phase(i, X_V), 0)]
        if 0 <= i < NTILE:
            ring += [("s", i, k) for k in chunks(i)]
        if weights_in(i) is not None:
            ring += [("w", weights_in(i), j) for j in range(2)]
    SLOT = {item: n for n, item in enumerate(ring)}

    turn = []
    for i in range(FIRST_STEP, STEPS):
        if i == SHARED_AT[0]:
            late = len(turn)
        if phase(i, X_T) is not None:
            turn.append(("x", phase(i, X_T), 0))
        if added_in(i) is not None:
            turn.append(("o", added_in(i), 0))
        if second(i, Y_GATE) is not None:
            turn.append(("g", second(i, Y_GATE), 0))
        if second(i, Y_T) is not None:
            turn.append(("y", second(i, Y_T), 0))
        if turned_in(i) is not None:
            turn += [("p", turned_in(i), k) for k in chunks(turned_in(i))]
    TURN_BANK, BEFORE, last_in = {}, {}, {}
    for n, item in enumerate(turn):
        at = RING + (n % TURNS if n < late else 1 + n % (TURNS - 1))
        TURN_BANK[item], BEFORE[item] = at, last_in.get(at)
        last_in[at] = item
    BEFORE["shared"] = last_in[RING]

    def on_act(c):
        return c % 2 == 0

    def act_turns(c):
        return sum(on_act(n) for n in range(c))

    def dve_turns(c):
        return c - act_turns(c)

    ROW_BU, ROW_BD = 0, SLOTS * FC
    ROW_GATE = ROW_BD + SLOTS
    ROWS = ROW_GATE + E
    assert ROWS <= P
    SA, CA, GA, SB, CB, GB = range(6)
    MOD_PART = [slice(0, 2), slice(2, 6)]

    w_dram = nc.dram_tensor("route_scratch", (NB, NT, E, P), F32, kind="Internal").ap()

    with ExitStack() as ctx:
        def sb(name, shape, dt=F32):
            return ctx.enter_context(nc.sbuf_tensor(name, shape, dt))

        def sem(name):
            return ctx.enter_context(nc.semaphore(name))

        bank = [ctx.enter_context(nc.psum_tensor(f"bank{i}", [P, BLOCK], F32)) for i in range(8)]

        ident = sb("ident", [P, P])
        ident_r = sb("ident_r", [P, P], F32R)
        mask = sb("mask", [P, P])
        mask_r = sb("mask_r", [P, P], F32R)
        rows = sb("rows", [P, P])
        cols = sb("cols", [P, ROWS])
        gate_b = sb("gate_b", [P, E])
        down_count = sb("down_count", [P, E])
        silu = sb("silu", [P, 4, NB])
        c_rows = sb("c_rows", [NB, P])
        mods = sb("mods", [P, 6 * NB])
        bias_now = sb("bias_now", [P, 2, FC])
        gsign = sb("gsign", [P, 2, NB])
        wqkv_hi = sb("wqkv_hi", [P, 3 * P], F32R)
        wqkv_lo = sb("wqkv_lo", [P, 3 * P], F32R)
        x_sb = sb("x_sb", [P, TILES * P])
        ln_const = sb("ln_const", [P, 4, TPB])
        EPS, MINUS_HALF, THREE_HALVES = range(3)
        stats = sb("stats", [P, 2, TPB, 6])
        moments = sb("moments", [P, 2, TPB, 2])
        ln_work = sb("ln_work", [P, 2, 4, TPB])
        rstd = sb("rstd", [P, 2, TPB])
        xn = sb("xn", [P, 2, BLOCK])
        xn2 = sb("xn2", [P, BLOCK])
        hT = sb("hT", [P, 2, BLOCK])
        hT_hi = sb("hT_hi", [P, 2, BLOCK], F32R)
        hT_lo = sb("hT_lo", [P, 2, BLOCK], F32R)
        h2T = sb("h2T", [P, BLOCK])
        h2_hi = sb("h2_hi", [P, TILES * P], F32R)
        h2_lo = sb("h2_lo", [P, TILES * P], F32R)
        kq_hi = sb("kq_hi", [P, TILES * P + QRING * BLOCK], F32R)
        kq_lo = sb("kq_lo", [P, TILES * P + QRING * BLOCK], F32R)
        v_sb = sb("v_sb", [P, SEQ])
        probs = sb("probs", [P, 2, SEQ])
        probsT = sb("probsT", [P, 2, NT * PAIR])
        chunk_max = sb("chunk_max", [P, 2, NQ])
        neg_max = sb("neg_max", [P, NTILE])
        exp_sum = sb("exp_sum", [P, NTILE, NQ])
        row_sum = sb("row_sum", [P, 2])
        row_inv = sb("row_inv", [P, 2])
        oT = sb("oT", [P, 2, PAIR])
        raw = sb("raw", [P, 2, 2, F])
        up_hi = sb("up_hi", [P, 2, F], F32R)
        up_lo = sb("up_lo", [P, 2, F], F32R)
        down_hi = sb("down_hi", [P, 2, FC * P], F32R)
        down_lo = sb("down_lo", [P, 2, FC * P], F32R)
        logits = sb("logits", [P, TILES * E])

        mod_raw = [bank[RING - 1][:, 0:6 * NB], bank[7][:, 0:6 * NB]]
        wmod_sb = probs[:, 0, 0:6 * P]
        wqkv = probs[:, 1, 0:3 * P]
        a_sb = probs[:, :, :]
        a_hi = kq_hi[:, 0:2 * FC * BLOCK].rearrange("p (u f) -> p u f", u=2)
        a_lo = kq_lo[:, 0:2 * FC * BLOCK].rearrange("p (u f) -> p u f", u=2)
        raw_up, raw_down = raw[:, 0, :, :], raw[:, 1, :, :]
        v_of = [v_sb[:, :], raw[:, :, :, :].rearrange("p j s f -> p (j s f)")]
        PCH = 2 * SEQ // BLOCK
        probs_at = probs[:, :, :].rearrange("p u (c k) -> p (u c) k", k=BLOCK)
        assert SEQ == FC * BLOCK and NT * PAIR == TILES * P and NB == 2
        acc = probsT[:, 0, :]
        w_bc = probsT[:, 1, :].rearrange("p (b t) -> p b t", b=NB)
        yw = xn
        accg = hT
        work = [v_sb[:, n * TILES * E:(n + 1) * TILES * E] for n in range(7)]
        score, tie, pick1, pick2 = (w.rearrange("p (n e) -> p n e", e=E) for w in work[0:4])
        weight = work[4]
        weightT = work[5].rearrange("p (b t) -> p b t", b=NB)
        best = work[6][:, 0:4 * TILES].rearrange("p (k n) -> p k n", k=4)

        x_in = [sem(f"x_in{n}") for n in range(NBLK)]
        c_in, c_T, biases_ready = sem("c_in"), sem("c_T"), sem("biases_ready")
        rows_in, qkv_in, gate_b_in = sem("rows_in"), sem("qkv_in"), sem("gate_b_in")
        wmod_in = [sem("wmod_in0"), sem("wmod_in1")]
        raw_in = [sem("raw_in0"), sem("raw_in1")]
        pool_ready = sem("pool_ready")
        consts_r = sem("consts_r")
        rows_T, cols_ready = sem("rows_T"), sem("cols_ready")
        silu_exp, silu_ready, mod_mm, mods_ready = sem("silu_exp"), sem("silu_ready"), sem("mod_mm"), sem("mods_ready")
        dve_step = sem("dve_step")
        moments_ready, rstd_ready = sem("moments_ready"), sem("rstd_ready")
        pool_step = sem("pool_step")
        xn_ready, xT_done = sem("xn_ready"), sem("xT_done")
        h_hi_done, h_lo_done = sem("h_hi_done"), sem("h_lo_done")
        qk_done, v_mm, qk_hi_done, qk_lo_done, v_done = sem("qk_done"), sem("v_mm"), sem("qk_hi_done"), sem("qk_lo_done"), sem("v_done")
        score_done, neg_max_ready, exp_done = sem("score_done"), sem("neg_max_ready"), sem("exp_done")
        pT_done, pT_act, pT_dve = sem("pT_done"), sem("pT_act"), sem("pT_dve")
        pv_done, oT_ready, oTT_done, x1_done = sem("pv_done"), sem("oT_ready"), sem("oTT_done"), sem("x1_done")
        x2n_ready, x2T_done, h2T_ready = sem("x2n_ready"), sem("x2T_done"), sem("h2T_ready")
        h2_lo_done, gate_done, logit_done = sem("h2_lo_done"), sem("gate_done"), sem("logit_done")
        sig_exp, weight_ready, weightT_mm, weightT_ready, weight_out = sem("sig_exp"), sem("weight_ready"), sem("weightT_mm"), sem("weightT_ready"), sem("weight_out")
        w_bc_in = [sem("w_bc_in0"), sem("w_bc_in1")]
        wT_done, w_hi_done, w_lo_done = sem("wT_done"), sem("w_hi_done"), sem("w_lo_done")
        a_hi_act = sem("a_hi_act")
        up_done, gelu_done, a_hi_done, a_lo_done = sem("up_done"), sem("gelu_done"), sem("a_hi_done"), sem("a_lo_done")
        START = 1
        down_done, yw_ready, acc_done = sem("down_done"), sem("yw_ready"), sem("acc_done")
        accg_ready, accT_done, out_ready, stored = sem("accg_ready"), sem("accT_done"), sem("out_ready"), sem("stored")

        x_tiles = x.rearrange("b (n p) d -> p b n d", p=P)
        out_tiles = out.rearrange("b (n p) d -> p b n d", p=P)
        x_view = x_sb[:, :].rearrange("p (b n d) -> p b n d", b=NB, n=NT)

        def tok(tile, n=1):
            return bass.ds(tile * P, n * P)

        def k_cols(n):
            b, q = BLOCKS[n]
            return slice(b * SEQ + q * BLOCK, b * SEQ + (q + 1) * BLOCK)

        def q_cols(n, tile=0, tiles=TPB):
            at = TILES * P + n % QRING * BLOCK + tile * P
            return slice(at, at + tiles * P)

        def mod(j, b):
            return mods[:, j * NB + b:j * NB + b + 1]

        def turn_bank(kind, i, k=0):
            return bank[TURN_BANK[kind, i, k]]

        def wmod_part(part):
            return slice(MOD_PART[part].start * P, MOD_PART[part].stop * P)

        block = ctx.enter_context(nc.Block())

        @block.sync
        def _(sync):
            def load_raw(s, up, down):
                sync.dma_start(raw_up[:, s % 2, :].rearrange("p (f h) -> p f h", f=FC),
                               up.rearrange("(f p) h -> p f h", p=P)).then_inc(raw_in[s % 2], 16)
                sync.dma_start(raw_down[:, s % 2, :], down).then_inc(raw_in[s % 2], 16)

            def load_x(n):
                b, q = BLOCKS[n]
                at = slice(q * TPB, (q + 1) * TPB)
                sync.dma_start(x_view[:, b, at, :], x_tiles[:, b, at, :]).then_inc(x_in[n], 16)

            load_x(0)
            load_raw(0, sWu, sWd)
            load_x(1)
            for at, src in ((ROW_BU, sbu.rearrange("(c f) -> c f", f=P)),
                            (ROW_BU + FC, bu.rearrange("e (c f) -> (e c) f", f=P)),
                            (ROW_BD, sbd.rearrange("(o h) -> o h", o=1)),
                            (ROW_BD + 1, bd), (ROW_GATE, gate_w)):
                sync.dma_start(rows[at:at + src.shape[0], :], src).then_inc(rows_in, 16)
            sync.dma_start(wmod_sb[:, wmod_part(1)], wmod[:, wmod_part(1)]).then_inc(wmod_in[1], 16)
            load_x(2)
            load_raw(1, Wu[0], Wd[0])
            sync.dma_start(gate_b[:, :], gate_bias.rearrange("(o e) -> o e", o=1).broadcast_to([P, E])
                           ).then_inc(gate_b_in, 16)
            for n in range(3, NBLK):
                load_x(n)
            sync.wait_ge(pv_done, NB * NPAIR)
            for s in (2, 3):
                load_raw(s, Wu[s - 1], Wd[s - 1])

            sync.wait_ge(weightT_ready, NB)
            sync.dma_start(w_dram.rearrange("b n e t -> (n e) b t"), weightT[:, :, :]).then_inc(weight_out, 16)
            sync.wait_ge(weight_out, 16)

            def load_weights_bc(s, e, b):
                sync.dma_start(w_bc[:, b, :].rearrange("p (n t) -> p n t", n=NT),
                               w_dram[b, :, e, :].rearrange("n (o t) -> o n t", o=1).broadcast_to([P, NT, P])
                               ).then_inc(w_bc_in[b], 16)

            for b in range(NB):
                load_weights_bc(1, 0, b)
            for s in range(2, SLOTS):
                if s + 2 < SLOTS:
                    sync.wait_ge(wT_done, 2 * s + 2)
                    load_raw(s + 2, Wu[s + 1], Wd[s + 1])
                for b in range(NB):
                    sync.wait_ge(yw_ready, START + NBLK * (s - 1) + NQ * (b + 1))
                    load_weights_bc(s, s - 1, b)

            for n in range(NBLK):
                b, q = n // NQ, n % NQ
                sync.wait_ge(out_ready, n + 1)
                sync.dma_start(out_tiles[:, b, TPB * q:TPB * (q + 1), :],
                               x_view[:, b, TPB * q:TPB * (q + 1), :]).then_inc(stored, 16)
            sync.wait_ge(stored, 16 * NBLK)

        @block.gpsimd
        def _(pool):
            pool.sem_inc(acc_done, START)
            nc.gpsimd.memset(ident[:, :], 0.0).then_inc(pool_ready, 1)
            for n, value in ((EPS, LN_EPS), (MINUS_HALF, -0.5), (THREE_HALVES, 1.5)):
                last = nc.gpsimd.memset(ln_const[:, n, :], value)
            last.then_inc(pool_ready, 1)
            nc.gpsimd.memset(mask[:, :], 0.0).then_inc(pool_ready, 1)
            nc.gpsimd.iota(down_count[:, :], pattern=[[-1, E]], base=E, channel_multiplier=0,
                           allow_small_or_imprecise_dtypes=True).then_inc(pool_ready, 1)
            pool.wait_ge(pool_ready, 4)
            nc.gpsimd.affine_select(out=ident[:, :], in_=ident[:, :], compare_op=ALU.not_equal, fill=1.0, base=0,
                                    pattern=[[-1, P]], channel_multiplier=1).then_inc(pool_ready, 1)
            nc.gpsimd.affine_select(out=mask[:, :], in_=mask[:, :], compare_op=ALU.is_ge, fill=MASKED, base=0,
                                    pattern=[[-1, P]], channel_multiplier=1).then_inc(pool_ready, 1)

            own, turns = Steps(), [0]

            def inverse_std(which):
                tt, k, var, r = nc.gpsimd.tensor_tensor, ln_const, moments[:, which, :, 1], rstd[:, which, :]
                v, guess, h, w = (ln_work[:, which, n, :] for n in range(4))
                turns[0] += 1
                pool.wait_ge(moments_ready, turns[0])
                tt(v, var, k[:, EPS, :], ALU.add).then_inc(pool_step, 1)
                pool.wait_ge(pool_step, own.next())
                tt(guess, v, k[:, MINUS_HALF, :], ALU.pow)
                tt(h, v, k[:, MINUS_HALF, :], ALU.mult).then_inc(pool_step, 1)
                pool.wait_ge(pool_step, own.next())
                tt(w, guess, guess, ALU.mult).then_inc(pool_step, 1)
                pool.wait_ge(pool_step, own.next())
                tt(w, w, h, ALU.mult).then_inc(pool_step, 1)
                pool.wait_ge(pool_step, own.next())
                tt(w, w, k[:, THREE_HALVES, :], ALU.add).then_inc(pool_step, 1)
                pool.wait_ge(pool_step, own.next())
                tt(r, w, guess, ALU.mult).then_inc(rstd_ready, 1)

            for i in range(FIRST_STEP, STEPS):
                if phase(i, X_STATS) is not None:
                    inverse_std(0)
                if second(i, Y_STATS) is not None:
                    inverse_std(1)

            with pool.Fori(1, SLOTS) as s:
                with pool.Fori(0, NQ) as half:
                    for par in range(2):
                        u = s * NBLK + half * 2 + par
                        at = bass.ds(half * (2 * BLOCK) + par * BLOCK, BLOCK)
                        pool.wait_ge(yw_ready, START + u + 1)
                        pool.wait_ge(acc_done, START + u - NBLK)
                        nc.gpsimd.tensor_tensor(acc[:, at], acc[:, at], yw[:, par, :], ALU.add).then_inc(acc_done, 1)

        @block.tensor
        def _(pe):
            def transpose4(dst, src, n=TPB):
                for t in range(n):
                    last = nc.tensor.transpose(dst[:, t * P:(t + 1) * P], src[:, t * P:(t + 1) * P], ident[:, :])
                return last

            def three(dst, w_hi, w_lo, m_hi, m_lo, start, stop):
                nc.tensor.matmul(dst, w_hi, m_hi, start=start, stop=False)
                nc.tensor.matmul(dst, w_hi, m_lo, start=False, stop=False)
                return nc.tensor.matmul(dst, w_lo, m_hi, start=False, stop=stop)

            def weights_T(s, loads, dst=lambda j: bank[5 + j]):
                pe.wait_ge(raw_in[s % 2], 32 * loads)
                for j, src in ((0, raw_up), (1, raw_down)):
                    transpose4(dst(j), src[:, s % 2, :], FC).then_inc(wT_done, 1)

            def rows_to_columns():
                pe.wait_ge(pool_ready, 6)
                pe.wait_ge(rows_in, 16 * 5)
                nc.tensor.transpose(bank[6][:, 0:ROWS], rows[0:ROWS, :], ident[0:ROWS, 0:ROWS]).then_inc(rows_T, 1)

            def modulation(part):
                pe.wait_ge(silu_ready, 1)
                pe.wait_ge(wmod_in[part], 16)
                for j in range(6)[MOD_PART[part]]:
                    last = nc.tensor.matmul(mod_raw[part][:, j * NB:(j + 1) * NB], wmod_sb[:, j * P:(j + 1) * P],
                                            silu[:, 3, :], start=True, stop=True)
                last.then_inc(mod_mm, 1)

            def wait_turn(item):
                if BEFORE[item]:
                    kind, i, k = BEFORE[item]
                    if kind == "x":
                        pe.wait_ge(h_hi_done, i + 1)
                    elif kind == "o":
                        pe.wait_ge(x1_done, i + 1)
                    elif kind == "y":
                        pe.wait_ge(h2T_ready, i + 1)
                    elif kind == "g":
                        pe.wait_ge(logit_done, i + 1)
                    elif on_act(CHUNK[i] + k):
                        pe.wait_ge(pT_act, act_turns(CHUNK[i] + k) + 1)
                    else:
                        pe.wait_ge(pT_dve, dve_turns(CHUNK[i] + k) + 1)

            def into(item):
                wait_turn(item)
                return turn_bank(*item)

            def wait_ring(item):
                n = SLOT[item]
                if n >= RING:
                    kind, i, k = ring[n - RING]
                    if kind == "v":
                        pe.wait_ge(v_done, i + 1)
                    elif kind == "s":
                        pe.wait_ge(exp_done, CHUNK[i] + k + 1)
                    elif kind == "w":
                        pe.wait_ge(w_lo_done, 2 * i + k + 1)
                    else:
                        pe.wait_ge(qk_lo_done, 2 * i + (kind == "k") + 1)
                return bank[n % RING]

            def x_T(n):
                pe.wait_ge(xn_ready, n + 1)
                if n == 1:
                    pe.wait_ge(cols_ready, 1)
                transpose4(into(("x", n, 0)), xn[:, n % 2, :]).then_inc(xT_done, 1)

            def project_qk(n):
                pe.wait_ge(h_lo_done, n + 1)
                if n == 0:
                    pe.wait_ge(consts_r, 3)
                for j in range(2):
                    w = slice(j * P, (j + 1) * P)
                    three(wait_ring(("qk"[j], n, 0))[:, :], wqkv_hi[:, w], wqkv_lo[:, w], hT_hi[:, n % 2, :],
                          hT_lo[:, n % 2, :], True, True).then_inc(qk_done, 1)

            def project_v(n):
                w = slice(2 * P, 3 * P)
                dst = wait_ring(("v", n, 0))
                for t in range(TPB):
                    ts = slice(t * P, (t + 1) * P)
                    last = three(dst[:, ts], hT_hi[:, n % 2, ts], hT_lo[:, n % 2, ts], wqkv_hi[:, w],
                                 wqkv_lo[:, w], True, True)
                last.then_inc(v_mm, 1)

            def scores(i):
                b, t = TILE[i]
                n = NUMBER[b, t // TPB]
                pe.wait_ge(qk_lo_done, 2 * n + 2)
                q_at = q_cols(n, t % TPB, 1)
                for k in chunks(i):
                    n = key_tiles(i, k) * P
                    dst = wait_ring(("s", i, k))
                    k_at = slice(b * SEQ + k * BLOCK, b * SEQ + k * BLOCK + n)
                    nc.tensor.matmul(dst[:, 0:n], kq_hi[:, q_at], kq_hi[:, k_at], start=True, stop=False)
                    if k == t // TPB:
                        nc.tensor.matmul(dst[:, n - P:n], ident_r[:, :], mask_r[:, :], start=False, stop=False)
                    nc.tensor.matmul(dst[:, 0:n], kq_hi[:, q_at], kq_lo[:, k_at], start=False, stop=False)
                    nc.tensor.matmul(dst[:, 0:n], kq_lo[:, q_at], kq_hi[:, k_at], start=False,
                                     stop=True).then_inc(score_done, 1)

            def probs_T(i):
                for k in chunks(i):
                    dst = into(("p", i, k))
                    pe.wait_ge(exp_done, CHUNK[i] + k + 1)
                    transpose4(dst, probs_at[:, (CHUNK[i] + k) % PCH, :], key_tiles(i, k)).then_inc(pT_done, 1)

            def pv(r, half):
                b, p = ORDER[r]
                if half == 0:
                    pe.wait_ge(v_done, NUMBER[b, p // 2] + 1)
                    if r:
                        pe.wait_ge(oT_ready, r)
                    else:
                        pe.wait_ge(mods_ready, 2)
                    pe.wait_ge(pT_act, act_turns(CHUNK[2 * r + 2]))
                    pe.wait_ge(pT_dve, dve_turns(CHUNK[2 * r + 2]))
                for j in range(half * (p + 1), (half + 1) * (p + 1)):
                    lo = P if j == 2 * p + 1 else 0
                    mm = nc.tensor.matmul(bank[7][:, lo:PAIR], v_of[b][:, j * P:(j + 1) * P],
                                          probsT[:, r % 2, j * PAIR + lo:(j + 1) * PAIR], start=(j == 0),
                                          stop=(j == 2 * p + 1))
                if half:
                    mm.then_inc(pv_done, 1)

            def o_T(r):
                dst = into(("o", r, 0))
                pe.wait_ge(oT_ready, r + 1)
                transpose4(dst, oT[:, r % 2, :], 2).then_inc(oTT_done, 1)

            def x2_T(n):
                dst = into(("y", n, 0))
                pe.wait_ge(x2n_ready, n + 1)
                transpose4(dst, xn2[:, :]).then_inc(x2T_done, 1)

            def gate(n):
                dst = into(("g", n, 0))
                pe.wait_ge(h2T_ready, n + 1)
                for t in range(TPB):
                    last = nc.tensor.matmul(dst[:, t * E:(t + 1) * E], h2T[:, t * P:(t + 1) * P],
                                            cols[:, ROW_GATE:ROW_GATE + E], start=True, stop=True)
                last.then_inc(gate_done, 1)

            def up(s, u, blk, at):
                for f in range(FC):
                    fs = slice(f * P, (f + 1) * P)
                    if not (isinstance(u, int) and u < 1):
                        pe.wait_ge(gelu_done, FC * u - FC + f + 1)
                    three(bank[f][:, :], up_hi[:, s % 2, fs], up_lo[:, s % 2, fs], h2_hi[:, bass.ds(at, BLOCK)],
                          h2_lo[:, bass.ds(at, BLOCK)], True, True).then_inc(up_done, 1)

            def down(s, u, par):
                if not (isinstance(u, int) and u < 2):
                    pe.wait_ge(yw_ready, START + u - 1)
                for f in range(FC):
                    if f % 2 == 0:
                        pe.wait_ge(a_lo_done, 2 * u + f // 2 + 1)
                    fs, at = slice(f * P, (f + 1) * P), slice(f * BLOCK, (f + 1) * BLOCK)
                    mm = three(bank[Y_BANK[par]][:, :], down_hi[:, s % 2, fs], down_lo[:, s % 2, fs],
                               a_hi[:, par, at], a_lo[:, par, at], f == 0, f == FC - 1)
                mm.then_inc(down_done, 1)

            def slot(s, base, n_slot, loads, prefetch):
                pe.wait_ge(w_lo_done, 2 * n_slot + 2)
                up(s, base, 0, 0)
                down(s + 1, base - 1, 1)
                up(s, base + 1, 1, BLOCK)
                down(s, base, 0)
                if prefetch:
                    weights_T(s + 1, loads)
                with pe.Fori(1, NBLK // 2) as it:
                    up(s, base + it * 2, 0, it * (2 * BLOCK))
                    down(s, base + it * 2 - 1, 1)
                    up(s, base + it * 2 + 1, 1, it * (2 * BLOCK) + BLOCK)
                    down(s, base + it * 2, 0)

            def shared_unit(n):
                if n == 0:
                    pe.wait_ge(w_lo_done, 2)
                if n == 1:
                    wait_turn("shared")
                pe.wait_ge(h2_lo_done, n + 1)
                up(0, n, n % 2, n * BLOCK)
                if n > 0:
                    down(0, n - 1, (n - 1) % 2)

            for i in range(FIRST_STEP, STEPS):
                if i == FIRST_STEP:
                    pe.wait_ge(pool_ready, 6)
                    pe.wait_ge(c_in, 16)
                    nc.tensor.transpose(bank[2][:, 0:NB], c_rows[:, :], ident[0:NB, 0:NB]).then_inc(c_T, 1)
                    modulation(0)
                if phase(i, X_T) is not None:
                    x_T(phase(i, X_T))
                if phase(i, X_QK) is not None:
                    project_qk(phase(i, X_QK))
                if phase(i, X_V) is not None:
                    project_v(phase(i, X_V))
                if 0 <= i < NTILE:
                    scores(i)
                if added_in(i) is not None:
                    o_T(added_in(i))
                if second(i, Y_GATE) is not None:
                    gate(second(i, Y_GATE))
                if second(i, Y_T) is not None:
                    x2_T(second(i, Y_T))
                if pv_of(i):
                    pv(*pv_of(i))
                if turned_in(i) is not None:
                    probs_T(turned_in(i))
                if i == STARTS[0]:
                    rows_to_columns()
                    modulation(1)
                if weights_in(i) is not None:
                    weights_T(weights_in(i), 1, lambda j: wait_ring(("w", weights_in(i), j)))
                if i in SHARED_AT:
                    shared_unit(SHARED_AT.index(i))

            pe.wait_ge(logit_done, NBLK)
            for n in range(len(SHARED_AT), NBLK):
                shared_unit(n)
                if n == NBLK - 2:
                    pe.wait_ge(weight_ready, 1)
                    for b in range(NB):
                        last = nc.tensor.transpose(bank[6][:, b * P:(b + 1) * P],
                                                   weight[:, b * NT * E:(b + 1) * NT * E], ident[:, :])
                    last.then_inc(weightT_mm, 1)
            pe.wait_ge(weightT_ready, NB)
            with pe.Fori(0, (SLOTS - 3) // 2) as pair:
                for par in (1, 2):
                    n = pair * 2 + par
                    slot(par, n * NBLK, n, pair + 2, True)
            slot(SLOTS - 2, (SLOTS - 2) * NBLK, SLOTS - 2, (SLOTS - 1) // 2 + 1, True)

            def sum_T(n):
                pe.wait_ge(accg_ready, n + 1)
                if n >= 2:
                    pe.wait_ge(out_ready, n - 1)
                transpose4(bank[5 + n % 2], accg[:, n % 2, :]).then_inc(accT_done, 1)

            base = (SLOTS - 1) * NBLK
            pe.wait_ge(w_lo_done, 2 * SLOTS)
            for n in range(NBLK):
                up(SLOTS - 1, base + n, n % 2, n * BLOCK)
                down(SLOTS - 1 if n else SLOTS - 2, base + n - 1, (n - 1) % 2)
                if n >= SUM_LAG:
                    sum_T(n - SUM_LAG)
            down(SLOTS - 1, base + NBLK - 1, 1)
            for n in range(NBLK - SUM_LAG, NBLK):
                sum_T(n)

        @block.scalar
        def _(act):
            act.dma_start(c_rows[:, :], c).then_inc(c_in, 16)
            act.dma_start(wmod_sb[:, wmod_part(0)], wmod[:, wmod_part(0)]).then_inc(wmod_in[0], 16)
            for j, w in enumerate((Wq, Wk, Wv)):
                act.dma_start(wqkv[:, j * P:(j + 1) * P], w).then_inc(qkv_in, 16)

            def weights_hi(s, n_slot, src=lambda j: bank[5 + j]):
                for j, dst in ((0, up_hi), (1, down_hi)):
                    act.wait_ge(wT_done, 2 * n_slot + j + 1)
                    nc.scalar.copy(dst[:, s % 2, :], src(j)[:, :]).then_inc(w_hi_done, 1)

            act.wait_ge(c_T, 1)
            nc.scalar.activation(silu[:, 0, :], bank[2][:, 0:NB], ACT.Exp, scale=-1.0).then_inc(silu_exp, 1)

            def h_hi(n):
                b = BLOCKS[n][0]
                act.wait_ge(xT_done, n + 1)
                if n >= 2:
                    act.wait_ge(h_lo_done, n - 1)
                    act.wait_ge(v_mm, n - 1)
                if n == 0:
                    act.wait_ge(mods_ready, 1)
                src = turn_bank("x", n)
                nc.scalar.activation(hT[:, n % 2, :], src[:, :], ACT.Identity, bias=mod(SA, b), scale=mod(CA, b))
                nc.scalar.activation(hT_hi[:, n % 2, :], src[:, :], ACT.Identity, bias=mod(SA, b),
                                     scale=mod(CA, b)).then_inc(h_hi_done, 1)

            def qk_high(n):
                act.wait_ge(qk_done, 2 * n + 1)
                if n >= QRING:
                    act.wait_ge(score_done, CHUNK[LAST_TILE[n - QRING] + 1])
                nc.scalar.activation(kq_hi[:, q_cols(n)], bank[SLOT["q", n, 0] % RING][:, :], ACT.Copy,
                                     scale=SCALE).then_inc(qk_hi_done, 1)
                act.wait_ge(qk_done, 2 * n + 2)
                nc.scalar.copy(kq_hi[:, k_cols(n)], bank[SLOT["k", n, 0] % RING][:, :]).then_inc(qk_hi_done, 1)

            def v_out(n):
                b, q = BLOCKS[n]
                act.wait_ge(v_mm, n + 1)
                nc.scalar.copy(v_of[b][:, q * BLOCK:(q + 1) * BLOCK],
                               bank[SLOT["v", n, 0] % RING][:, :]).then_inc(v_done, 1)

            def exps(i, k):
                c = CHUNK[i] + k
                if k == 0:
                    act.wait_ge(neg_max_ready, i + 1)
                if c >= PCH:
                    act.wait_ge(pT_done, c - PCH + 1)
                n = key_tiles(i, k) * P
                nc.scalar.activation(probs_at[:, c % PCH, 0:n], bank[SLOT["s", i, k] % RING][:, 0:n], ACT.Exp,
                                     bias=neg_max[:, i:i + 1],
                                     accum_out=exp_sum[:, i, k:k + 1]).then_inc(exp_done, 1)

            def probs_out(i, k):
                c = CHUNK[i] + k
                act.wait_ge(pT_done, c + 1)
                if i >= 4:
                    act.wait_ge(pv_done, i // 2 - 1)
                n = key_tiles(i, k)
                at = i % 2 * P
                dst = probsT[:, i // 2 % 2, :].rearrange("p (j t) -> p j t", t=PAIR)
                src = turn_bank("p", i, k)[:, 0:n * P].rearrange("p (j t) -> p j t", t=P)
                nc.scalar.copy(dst[:, TPB * k:TPB * k + n, at:at + P], src).then_inc(pT_act, 1)

            def o_out(r):
                act.wait_ge(pv_done, r + 1)
                if r == 0:
                    act.wait_ge(mods_ready, 2)
                if r >= 2:
                    act.wait_ge(oTT_done, r - 1)
                nc.scalar.activation(oT[:, r % 2, :], bank[7][:, 0:PAIR], ACT.Copy,
                                     scale=mod(GA, ORDER[r][0])).then_inc(oT_ready, 1)

            def h2(n):
                b, q = DONE[n]
                act.wait_ge(x2T_done, n + 1)
                if n >= 1:
                    act.wait_ge(gate_done, n)
                    act.wait_ge(h2_lo_done, n)
                src = turn_bank("y", n)
                nc.scalar.activation(h2T[:, :], src[:, :], ACT.Identity, bias=mod(SB, b), scale=mod(CB, b))
                nc.scalar.activation(h2_hi[:, tok(b * NT + q * TPB, TPB)], src[:, :], ACT.Identity,
                                     bias=mod(SB, b), scale=mod(CB, b)).then_inc(h2T_ready, 1)

            def gelus(s, u, par):
                for f in range(FC):
                    act.wait_ge(up_done, FC * u + f + 1)
                    if f % 2 == 0 and not (isinstance(u, int) and u < 2):
                        act.wait_ge(a_lo_done, 2 * u + f // 2 - 3)
                    nc.scalar.activation(a_sb[:, par, f * BLOCK:(f + 1) * BLOCK], bank[f][:, :], ACT.Gelu,
                                         bias=bias_now[:, s % 2, f:f + 1]).then_inc(gelu_done, 1)

            def shared_unit(n):
                if n == 0:
                    act.wait_ge(biases_ready, 1)
                gelus(0, n, n % 2)
                if n >= 2:
                    act.wait_ge(down_done, n - 1)
                act.wait_ge(gelu_done, FC * (n + 1))
                nc.scalar.copy(a_hi[:, n % 2, 2 * BLOCK:4 * BLOCK], a_sb[:, n % 2, 2 * BLOCK:4 * BLOCK]).then_inc(a_hi_act, 1)

            for i in range(FIRST_STEP, STEPS):
                if phase(i, X_T) is not None:
                    h_hi(phase(i, X_T))
                if phase(i, X_QK) is not None:
                    qk_high(phase(i, X_QK))
                if phase(i, X_V) is not None:
                    v_out(phase(i, X_V))
                if added_in(i) is not None:
                    o_out(added_in(i))
                if second(i, Y_T) is not None:
                    h2(second(i, Y_T))
                t = turned_in(i)
                for k in range(NQ + EXP_LEAD):
                    if 0 <= i < NTILE and k in chunks(i):
                        exps(i, k)
                    if t is not None and k - EXP_LEAD in chunks(t) and on_act(CHUNK[t] + k - EXP_LEAD):
                        probs_out(t, k - EXP_LEAD)
                s = weights_in(i)
                if s is not None:
                    weights_hi(s, s, lambda j: bank[SLOT["w", s, j] % RING])
                if i in SHARED_AT:
                    shared_unit(SHARED_AT.index(i))

            act.wait_ge(logit_done, NBLK)
            nc.scalar.activation(work[0], logits[:, :], ACT.Exp, scale=-1.0).then_inc(sig_exp, 1)
            for n in range(len(SHARED_AT), NBLK):
                shared_unit(n)

            def slot(s, base, n_slot, prefetch):
                act.wait_ge(w_lo_done, 2 * n_slot + 2)
                gelus(s, base, 0)
                gelus(s, base + 1, 1)
                if prefetch:
                    act.wait_ge(down_done, base)
                    weights_hi(s + 1, n_slot + 1)
                with act.Fori(1, NBLK // 2) as it:
                    for par in range(2):
                        gelus(s, base + it * 2 + par, par)

            with act.Fori(0, (SLOTS - 3) // 2) as pair:
                for par in (1, 2):
                    slot(par, (pair * 2 + par) * NBLK, pair * 2 + par, True)
            slot(SLOTS - 2, (SLOTS - 2) * NBLK, SLOTS - 2, True)

            def scale_sum(n):
                act.wait_ge(acc_done, START + (SLOTS - 2) * NBLK + n + 1)
                if n >= 2:
                    act.wait_ge(accT_done, n - 1)
                nc.scalar.activation(accg[:, n % 2, :], acc[:, n * BLOCK:(n + 1) * BLOCK], ACT.Copy,
                                     scale=mod(GB, n // NQ)).then_inc(accg_ready, 1)

            act.wait_ge(w_lo_done, 2 * SLOTS)
            for n in range(NBLK):
                gelus(SLOTS - 1, (SLOTS - 1) * NBLK + n, n % 2)
                if n >= SUM_LAG:
                    scale_sum(n - SUM_LAG)
            for n in range(NBLK - SUM_LAG, NBLK):
                scale_sum(n)

        @block.vector
        def _(dve):
            dve.sem_inc(yw_ready, START)

            def weights_lo(s, n_slot, src=lambda j: bank[5 + j]):
                if not isinstance(n_slot, int) or n_slot > 1:
                    nc.vector.tensor_copy(bias_now[:, s % 2, :], cols[:, bass.ds(n_slot * FC + ROW_BU, FC)])
                for j, hi, lo in ((0, up_hi, up_lo), (1, down_hi, down_lo)):
                    dve.wait_ge(w_hi_done, 2 * n_slot + j + 1)
                    nc.vector.tensor_tensor(lo[:, s % 2, :], src(j)[:, :], hi[:, s % 2, :].bitcast(F32),
                                            ALU.subtract).then_inc(w_lo_done, 1)

            step = Steps()

            dve.wait_ge(pool_ready, 6)
            nc.vector.tensor_copy(ident_r[:, :], ident[:, :]).then_inc(consts_r, 1)
            nc.vector.tensor_copy(mask_r[:, :], mask[:, :])

            def silu_of_c():
                dve.wait_ge(silu_exp, 1)
                nc.vector.tensor_scalar(silu[:, 1, :], silu[:, 0, :], 1.0, None, ALU.add).then_inc(dve_step, 1)
                dve.wait_ge(dve_step, step.next())
                nc.vector.reciprocal(silu[:, 2, :], silu[:, 1, :]).then_inc(dve_step, 1)
                dve.wait_ge(dve_step, step.next())
                nc.vector.tensor_tensor(silu[:, 3, :], silu[:, 2, :], bank[2][:, 0:NB], ALU.mult).then_inc(silu_ready, 1)

            def columns():
                dve.wait_ge(rows_T, 1)
                nc.vector.tensor_copy(cols[:, :], bank[6][:, 0:ROWS]).then_inc(cols_ready, 1)
                dve.wait_ge(cols_ready, 1)
                nc.vector.tensor_copy(bias_now[:, :, :], cols[:, ROW_BU:ROW_BU + 2 * FC].rearrange("p (s f) -> p s f", s=2)
                                      ).then_inc(biases_ready, 1)

            def projection_weights():
                dve.wait_ge(qkv_in, 48)
                nc.vector.tensor_copy(wqkv_hi[:, :], wqkv[:, :]).then_inc(consts_r, 1)
                dve.wait_ge(consts_r, 2)
                nc.vector.tensor_tensor(wqkv_lo[:, :], wqkv[:, :], wqkv_hi[:, :].bitcast(F32), ALU.subtract).then_inc(consts_r, 1)

            def shift_and_scale(src, shift, scale):
                nc.vector.tensor_copy(mods[:, shift * NB:(shift + 1) * NB], src[:, shift * NB:(shift + 1) * NB])
                return nc.vector.tensor_scalar(mods[:, scale * NB:(scale + 1) * NB], src[:, scale * NB:(scale + 1) * NB],
                                               1.0, None, ALU.add)

            def first_mods():
                dve.wait_ge(mod_mm, 1)
                shift_and_scale(mod_raw[0], SA, CA).then_inc(mods_ready, 1)

            def other_mods():
                dve.wait_ge(mod_mm, 2)
                shift_and_scale(mod_raw[1], SB, CB)
                assert (GA, GB) == (2, 5)
                gates, raw_gates = (ap.rearrange("p (g j b) -> p g j b", g=2, b=NB)[:, :, GA, :] for ap in (mods[:, :], mod_raw[1]))
                nc.vector.tensor_scalar(gsign[:, :, :], raw_gates, 0.0, 2.0, ALU.is_ge, ALU.mult).then_inc(dve_step, 1)
                dve.wait_ge(dve_step, step.next())
                nc.vector.tensor_scalar(gsign[:, :, :], gsign[:, :, :], -1.0, None, ALU.add).then_inc(dve_step, 1)
                dve.wait_ge(dve_step, step.next())
                nc.vector.tensor_tensor(gates, gsign[:, :, :], raw_gates, ALU.mult).then_inc(dve_step, 1)
                dve.wait_ge(dve_step, step.next())
                nc.vector.scalar_tensor_tensor(out=gates, in0=gates, scalar=0.25, in1=gsign[:, :, :],
                                               op0=ALU.max, op1=ALU.mult).then_inc(mods_ready, 1)

            def signal(instruction):
                instruction.then_inc(dve_step, 1)
                return step.next()

            turns, pending = [0], {}

            def take_statistics(which, b, q):
                for t in range(TPB):
                    last = nc.vector.bn_stats(stats[:, which, t, :], x_sb[:, tok(b * NT + q * TPB + t)])
                pending["stats", which] = signal(last)

            def take_moments(which):
                dve.wait_ge(dve_step, pending.pop(("stats", which)))
                for t in range(TPB):
                    last = nc.vector.bn_aggr(moments[:, which, t, :], stats[:, which, t, :])
                last.then_inc(moments_ready, 1)
                turns[0] += 1
                pending["rstd", which] = turns[0]

            def normalise(dst, which, b, q):
                dve.wait_ge(rstd_ready, pending.pop(("rstd", which)))
                for t in range(TPB):
                    last = nc.vector.tensor_scalar(dst[:, t * P:(t + 1) * P], x_sb[:, tok(b * NT + q * TPB + t)],
                                                   moments[:, which, t, 0:1], rstd[:, which, t:t + 1],
                                                   ALU.subtract, ALU.mult)
                return last

            def x_statistics(n):
                dve.wait_ge(x_in[n], 16)
                take_statistics(0, *BLOCKS[n])

            def x_norm(n):
                if n >= 2:
                    dve.wait_ge(xT_done, n - 1)
                normalise(xn[:, n % 2, :], 0, *BLOCKS[n]).then_inc(xn_ready, 1)

            def h_low(n):
                dve.wait_ge(h_hi_done, n + 1)
                if n >= 2:
                    dve.wait_ge(v_mm, n - 1)
                nc.vector.tensor_tensor(hT_lo[:, n % 2, :], hT[:, n % 2, :], hT_hi[:, n % 2, :].bitcast(F32),
                                        ALU.subtract).then_inc(h_lo_done, 1)

            def qk_low(n):
                at = q_cols(n)
                dve.wait_ge(qk_hi_done, 2 * n + 1)
                nc.vector.scalar_tensor_tensor(out=kq_lo[:, at], in0=bank[SLOT["q", n, 0] % RING][:, :], scalar=SCALE,
                                               in1=kq_hi[:, at].bitcast(F32), op0=ALU.mult,
                                               op1=ALU.subtract).then_inc(qk_lo_done, 1)
                at = k_cols(n)
                dve.wait_ge(qk_hi_done, 2 * n + 2)
                nc.vector.tensor_tensor(kq_lo[:, at], bank[SLOT["k", n, 0] % RING][:, :],
                                        kq_hi[:, at].bitcast(F32), ALU.subtract).then_inc(qk_lo_done, 1)

            def row_max(i):
                many = len(chunks(i)) > 1
                for k in chunks(i):
                    n = key_tiles(i, k) * P
                    dve.wait_ge(score_done, CHUNK[i] + k + 1)
                    dst = chunk_max[:, i % 2, k:k + 1] if many else neg_max[:, i:i + 1]
                    last = nc.vector.tensor_reduce(dst, bank[SLOT["s", i, k] % RING][:, 0:n], AX_X, ALU.max,
                                                   negate=not many)
                if many:
                    dve.wait_ge(dve_step, signal(last))
                    last = nc.vector.tensor_reduce(neg_max[:, i:i + 1], chunk_max[:, i % 2, 0:len(chunks(i))], AX_X,
                                                   ALU.max, negate=True)
                last.then_inc(neg_max_ready, 1)

            def probs_out(i, k):
                c = CHUNK[i] + k
                dve.wait_ge(pT_done, c + 1)
                if i >= 4:
                    dve.wait_ge(pv_done, i // 2 - 1)
                n = key_tiles(i, k)
                at = i % 2 * P
                dst = probsT[:, i // 2 % 2, :].rearrange("p (j t) -> p j t", t=PAIR)
                src = turn_bank("p", i, k)[:, 0:n * P].rearrange("p (j t) -> p j t", t=P)
                nc.vector.tensor_copy(dst[:, TPB * k:TPB * k + n, at:at + P], src).then_inc(pT_dve, 1)

            def residual(r):
                b, p = ORDER[r]
                dve.wait_ge(dve_step, pending.pop("inv"))
                dve.wait_ge(oTT_done, r + 1)
                src = turn_bank("o", r)
                for t in range(2):
                    at = tok(b * NT + 2 * p + t)
                    last = nc.vector.scalar_tensor_tensor(out=x_sb[:, at], in0=src[:, t * P:(t + 1) * P],
                                                          scalar=row_inv[:, t:t + 1], in1=x_sb[:, at],
                                                          op0=ALU.mult, op1=ALU.add)
                last.then_inc(x1_done, 1)

            def x2_statistics(n):
                b, q = DONE[n]
                dve.wait_ge(x1_done, ORDER.index((b, 2 * q + 1)) + 1)
                take_statistics(1, b, q)

            def x2_norm(n):
                if n >= 1:
                    dve.wait_ge(x2T_done, n)
                normalise(xn2[:, :], 1, *DONE[n]).then_inc(x2n_ready, 1)

            def h2_low(n):
                b, q = DONE[n]
                at = tok(b * NT + q * TPB, TPB)
                dve.wait_ge(h2T_ready, n + 1)
                nc.vector.tensor_tensor(h2_lo[:, at], h2T[:, :], h2_hi[:, at].bitcast(F32),
                                        ALU.subtract).then_inc(h2_lo_done, 1)

            def logits_out(n):
                b, q = DONE[n]
                dve.wait_ge(gate_done, n + 1)
                if n == 0:
                    dve.wait_ge(gate_b_in, 16)
                at = slice((b * NQ + q) * TPB * E, (b * NQ + q + 1) * TPB * E)
                nc.vector.tensor_tensor(logits[:, at].rearrange("p (n e) -> p n e", e=E),
                                        turn_bank("g", n)[:, 0:TPB * E].rearrange("p (n e) -> p n e", e=E),
                                        gate_b[:, :].rearrange("p (o e) -> p o e", o=1).broadcast_to([P, TPB, E]),
                                        ALU.add).then_inc(logit_done, 1)

            def per_expert(ap):
                return ap.rearrange("p (n o) -> p n o", o=1).broadcast_to([P, TILES, E])

            count = down_count[:, :].rearrange("p (o e) -> p o e", o=1).broadcast_to([P, TILES, E])

            def route_scores():
                dve.wait_ge(sig_exp, 1)
                nc.vector.tensor_scalar(score, score, 1.0, None, ALU.add).then_inc(dve_step, 1)
                dve.wait_ge(dve_step, step.next())
                nc.vector.reciprocal(score, score).then_inc(dve_step, 1)
                dve.wait_ge(dve_step, step.next())

            def route_pick(n, pick):
                top, who = best[:, n, :], best[:, 2, :]
                nc.vector.tensor_reduce(top, score, AX_X, ALU.max).then_inc(dve_step, 1)
                dve.wait_ge(dve_step, step.next())
                nc.vector.tensor_tensor(tie, score, per_expert(top), ALU.is_equal).then_inc(dve_step, 1)
                dve.wait_ge(dve_step, step.next())
                nc.vector.tensor_tensor(tie, tie, count, ALU.mult).then_inc(dve_step, 1)
                dve.wait_ge(dve_step, step.next())
                nc.vector.tensor_reduce(who, tie, AX_X, ALU.max).then_inc(dve_step, 1)
                dve.wait_ge(dve_step, step.next())
                nc.vector.tensor_tensor(pick, tie, per_expert(who), ALU.is_equal).then_inc(dve_step, 1)
                dve.wait_ge(dve_step, step.next())
                if n == 0:
                    nc.vector.scalar_tensor_tensor(out=score, in0=pick, scalar=-4.0, in1=score, op0=ALU.mult,
                                                   op1=ALU.add).then_inc(dve_step, 1)
                    dve.wait_ge(dve_step, step.next())

            def route_weights():
                nc.vector.tensor_tensor(best[:, 2, :], best[:, 0, :], best[:, 1, :], ALU.add).then_inc(dve_step, 1)
                dve.wait_ge(dve_step, step.next())
                nc.vector.tensor_scalar(best[:, 2, :], best[:, 2, :], 1e-6, None, ALU.add).then_inc(dve_step, 1)
                dve.wait_ge(dve_step, step.next())
                nc.vector.reciprocal(best[:, 3, :], best[:, 2, :]).then_inc(dve_step, 1)
                dve.wait_ge(dve_step, step.next())
                for n in range(2):
                    last = nc.vector.tensor_tensor(best[:, n, :], best[:, n, :], best[:, 3, :], ALU.mult)
                last.then_inc(dve_step, 1)
                dve.wait_ge(dve_step, step.next())
                for n, pick in enumerate((pick1, pick2)):
                    last = nc.vector.tensor_tensor(pick, pick, per_expert(best[:, n, :]), ALU.mult)
                last.then_inc(dve_step, 1)
                dve.wait_ge(dve_step, step.next())
                nc.vector.tensor_tensor(weight.rearrange("p (n e) -> p n e", e=E), pick1, pick2,
                                        ALU.add).then_inc(weight_ready, 1)

            def split(u, par, helped=False):
                for h in range(FC // 2):
                    at = slice(h * 2 * BLOCK, (h + 1) * 2 * BLOCK)
                    dve.wait_ge(gelu_done, FC * u + 2 * h + 2)
                    if h == 0 and not (isinstance(u, int) and u < 2):
                        dve.wait_ge(down_done, u - 1)
                    if helped and h == 1:
                        dve.wait_ge(a_hi_act, u + 1)
                    else:
                        chunk = u + 1 if helped else 2 * u + h + 1 - NBLK
                        nc.vector.tensor_copy(a_hi[:, par, at], a_sb[:, par, at]).then_inc(a_hi_done, 1)
                        dve.wait_ge(a_hi_done, chunk)
                    nc.vector.tensor_tensor(a_lo[:, par, at], a_sb[:, par, at], a_hi[:, par, at].bitcast(F32),
                                            ALU.subtract).then_inc(a_lo_done, 1)

            def weigh(u, par, blk, n_slot, shared):
                dve.wait_ge(down_done, u + 1)
                bias = cols[:, bass.ds(n_slot + ROW_BD, 1)]
                if shared:
                    nc.vector.tensor_scalar(acc[:, bass.ds(blk * BLOCK, BLOCK)], bank[Y_BANK[par]][:, :], bias, 0.1,
                                            ALU.add, ALU.mult).then_inc(yw_ready, 1)
                else:
                    if not (isinstance(u, int) and u < NBLK + 2):
                        dve.wait_ge(acc_done, START + u - NBLK - 1)
                    w = w_bc[:, :, :].rearrange("p b t -> p (b t)")[:, bass.ds(blk * BLOCK, BLOCK)]
                    nc.vector.scalar_tensor_tensor(out=yw[:, par, :], in0=bank[Y_BANK[par]][:, :], scalar=bias, in1=w,
                                                   op0=ALU.add, op1=ALU.mult).then_inc(yw_ready, 1)

            def slot(s, base, n_slot, prefetch, after_shared=False):
                split(base, 0)
                weigh(base - 1, 1, NBLK - 1, n_slot - 1, after_shared)
                split(base + 1, 1)
                dve.wait_ge(w_bc_in[0], n_slot * 16)
                weigh(base, 0, 0, n_slot, False)
                if prefetch:
                    weights_lo(s + 1, n_slot + 1)
                with dve.Fori(1, NBLK // 2) as it:
                    split(base + it * 2, 0)
                    weigh(base + it * 2 - 1, 1, it * 2 - 1, n_slot, False)
                    dve.wait_ge(w_bc_in[1], n_slot * 16)
                    split(base + it * 2 + 1, 1)
                    weigh(base + it * 2, 0, it * 2, n_slot, False)

            def shared_unit(n):
                split(n, n % 2, True)
                if n > 0:
                    weigh(n - 1, (n - 1) % 2, n - 1, 0, True)

            for i in range(FIRST_STEP, STEPS):
                r = added_in(i)
                if r is not None:
                    dve.wait_ge(exp_done, CHUNK[2 * r + 2])
                    pending["sum"] = signal(nc.vector.reduce_sum(row_sum[:, :], exp_sum[:, 2 * r:2 * r + 2, 0:len(chunks(2 * r))], AX_X))
                if phase(i, X_NORM) is not None:
                    x_norm(phase(i, X_NORM))
                if phase(i, X_T) is not None:
                    h_low(phase(i, X_T))
                if phase(i, X_QK) is not None:
                    qk_low(phase(i, X_QK))
                if second(i, Y_NORM) is not None:
                    x2_norm(second(i, Y_NORM))
                if 0 <= i < NTILE:
                    row_max(i)
                if r is not None:
                    dve.wait_ge(dve_step, pending.pop("sum"))
                    pending["inv"] = signal(nc.vector.reciprocal(row_inv[:, :], row_sum[:, :]))
                if phase(i, X_STATS) is not None:
                    x_statistics(phase(i, X_STATS))
                if r is not None:
                    residual(r)
                if second(i, Y_STATS) is not None:
                    x2_statistics(second(i, Y_STATS))
                if phase(i, X_STATS) is not None:
                    take_moments(0)
                if second(i, Y_GATE) is not None:
                    h2_low(second(i, Y_GATE))
                    logits_out(second(i, Y_GATE))
                t = turned_in(i)
                if t is not None:
                    for k in chunks(t):
                        if not on_act(CHUNK[t] + k):
                            probs_out(t, k)
                if second(i, Y_STATS) is not None:
                    take_moments(1)
                s = weights_in(i)
                if s is not None:
                    weights_lo(s, s, lambda j: bank[SLOT["w", s, j] % RING])
                if i == STARTS[0] - 3:
                    silu_of_c()
                    projection_weights()
                    first_mods()
                if i == STARTS[0]:
                    columns()
                    other_mods()
                if i in SHARED_AT:
                    shared_unit(SHARED_AT.index(i))

            for n in range(len(SHARED_AT), NBLK):
                shared_unit(n)
                if n == len(SHARED_AT):
                    route_scores()
                    route_pick(0, pick1)
                elif n == len(SHARED_AT) + 1:
                    route_pick(1, pick2)
                    route_weights()
            dve.wait_ge(weightT_mm, 1)
            for b in range(NB):
                nc.vector.tensor_copy(weightT[:, b, :], bank[6][:, b * P:(b + 1) * P]).then_inc(weightT_ready, 1)
            slot(1, NBLK, 1, True, after_shared=True)
            with dve.Fori(0, (SLOTS - 3) // 2) as pair:
                for par in (2, 3):
                    slot(par, (pair * 2 + par) * NBLK, pair * 2 + par, True)

            def add_sum(n):
                dve.wait_ge(accT_done, n + 1)
                at = slice(n * BLOCK, (n + 1) * BLOCK)
                nc.vector.tensor_tensor(x_sb[:, at], bank[5 + n % 2][:, :], x_sb[:, at], ALU.add).then_inc(out_ready, 1)

            base, n_slot = (SLOTS - 1) * NBLK, SLOTS - 1
            for n in range(NBLK):
                split(base + n, n % 2)
                if n % NQ == 1:
                    dve.wait_ge(w_bc_in[n // NQ], n_slot * 16)
                weigh(base + n - 1, (n - 1) % 2, (n - 1) % NBLK, n_slot if n else n_slot - 1, False)
                if n >= SUM_LAG:
                    add_sum(n - SUM_LAG)
            weigh(base + NBLK - 1, 1, NBLK - 1, n_slot, False)
            for n in range(NBLK - SUM_LAG, NBLK):
                add_sum(n)


_INS = ['L0_attn_x', 'L0_attn_Wk', 'L0_attn_Wq', 'L0_attn_Wv', 'L0_ffn_gate_w', 'L0_ffn_gate_bias', 'L0_ffn_Wu',
        'L0_ffn_bu', 'L0_ffn_Wd', 'L0_ffn_bd', 'L0_ffn_sWu', 'L0_ffn_sbu', 'L0_ffn_sWd', 'L0_ffn_sbd', 'L0_c', 'L0_wmod']


def kernel(**inputs):
    import numpy as _np
    import concourse.bacc as _bacc
    from concourse import mybir as _mybir
    from concourse.bass_utils import run_bass_kernel_spmd as _run

    nc = _bacc.Bacc("TRN2", target_bir_lowering=False, num_devices=1)
    arrays, args = {}, []
    for name in _INS:
        a = _np.ascontiguousarray(inputs[name])
        arrays[f"in_{name}_dram"] = a
        args.append(nc.dram_tensor(f"in_{name}_dram", a.shape, _mybir.dt.from_np(a.dtype), kind="ExternalInput").ap())
    shape = inputs["L0_attn_x"].shape
    args.append(nc.dram_tensor("out_0_dram", shape, _mybir.dt.float32, kind="ExternalOutput").ap())
    adaln_attention_moe(nc, *args)
    r = _run(nc, [arrays], core_ids=[0])
    return r.results[0]["out_0_dram"]
```

```python
from contextlib import ExitStack

import concourse.bass as bass
from concourse import mybir

ALU = mybir.AluOpType
ACT = mybir.ActivationFunctionType
F32 = mybir.dt.float32
F32R = mybir.dt.float32r
AX_X = mybir.AxisListType.X

P = 128
BLOCK = 512
TPB = BLOCK // P
MASKED = -1.0e30
LN_EPS = 1e-5




class Steps:

    def __init__(self, base=0):
        self.base, self.n = base, 0

    def next(self):
        self.n += 1
        return self.base + self.n


def adaln_attention_moe(nc, x, Wk, Wq, Wv, gate_w, gate_bias, Wu, bu, Wd, bd, sWu, sbu, sWd, sbd, c, wmod, out):
    NB, SEQ, D = x.shape
    E, F, _ = Wu.shape
    assert D == P and SEQ % BLOCK == 0 and F % P == 0
    NT = SEQ // P
    NQ = SEQ // BLOCK
    TILES = NB * NT
    FC = F // P
    SLOTS = E + 1
    NBLK = NB * NQ
    SUM_LAG = 3
    SCALE = float(D) ** -0.5

    PAIR = 2 * P
    PAIRS = TILES // 2

    def chunks(i):
        return range(i % NT // TPB + 1)

    def key_tiles(i, k):
        t = i % NT
        return TPB if k < t // TPB else t % TPB + 1

    CHUNK = [0]
    for i in range(TILES):
        CHUNK.append(CHUNK[-1] + len(chunks(i)))

    TURN_LAG = 1
    EXP_LEAD = 1

    def turned_in(i):
        return i - TURN_LAG if 0 <= i - TURN_LAG < TILES else None

    def pv_of(i):
        n = i - 2 - TURN_LAG
        return (n // 2, n % 2) if 0 <= n < TILES else None

    def added_at(r):
        return 2 * r + 4 + TURN_LAG

    def added_in(i):
        n = i - 4 - TURN_LAG
        return n // 2 if n % 2 == 0 and 0 <= n < TILES else None

    PROJECT_AHEAD = 4
    STARTS = [n * TPB - PROJECT_AHEAD for n in range(NBLK)]
    STARTS[1] = STARTS[0] + 2
    QRING = 3
    assert all((n - QRING + 1) * TPB <= STARTS[n] + 1 for n in range(QRING, NBLK))

    def phase(i, lag):
        return STARTS.index(i - lag) if i - lag in STARTS else None

    DONE_AT = [added_at(2 * n + 1) for n in range(NBLK)]

    def second(i, lag):
        return DONE_AT.index(i - lag) if i - lag in DONE_AT else None

    ROUTED_EARLY = 5
    ROUTE_TILES = [slice(0, ROUTED_EARLY * TPB), slice(ROUTED_EARLY * TPB, TILES)]
    ROUTES = len(ROUTE_TILES)

    X_STATS, X_NORM, X_T, X_QK, X_V = -4, -1, 0, 1, 2
    Y_STATS, Y_NORM, Y_T, Y_GATE = 0, 2, 3, 4
    FIRST_STEP = STARTS[0] + X_STATS
    STEPS = DONE_AT[-1] + Y_GATE + 1

    NORMS = []
    for i in range(FIRST_STEP, STEPS):
        if phase(i, X_STATS) is not None:
            NORMS.append(("x", phase(i, X_STATS)))
        if second(i, Y_STATS) is not None:
            NORMS.append(("y", second(i, Y_STATS)))

    def norm_place(norm):
        return norm[1] % 2 if norm[0] == "x" else 2

    def norm_count(norm):
        return NORMS.index(norm) + 1

    ROUTE_AT = DONE_AT[ROUTED_EARLY - 1] + Y_GATE + 1
    assert ROUTE_AT > DONE_AT[NQ - 1]

    WEIGHTS_0, WEIGHTS_1 = -1, 7
    assert WEIGHTS_1 < STARTS[NQ] + X_V

    def weights_in(i):
        return {WEIGHTS_0: 0, WEIGHTS_1: 1}.get(i)

    SHARED_AT = [TILES + TURN_LAG, DONE_AT[-1], DONE_AT[-1] + Y_NORM, DONE_AT[-1] + Y_T]
    Y_BANK = (4, 7)

    RING, TURNS = 4, 3
    ring = []
    for i in range(FIRST_STEP, STEPS):
        if phase(i, X_QK) is not None:
            ring += [("q", phase(i, X_QK), 0), ("k", phase(i, X_QK), 0)]
        if phase(i, X_V) is not None:
            ring += [("v", phase(i, X_V), 0)]
        if 0 <= i < TILES:
            ring += [("s", i, k) for k in chunks(i)]
        if weights_in(i) is not None:
            ring += [("w", weights_in(i), j) for j in range(2)]
    SLOT = {item: n for n, item in enumerate(ring)}

    turn = []
    for i in range(FIRST_STEP, STEPS):
        if i == SHARED_AT[0]:
            late = len(turn)
        if phase(i, X_T) is not None:
            turn.append(("x", phase(i, X_T), 0))
        if added_in(i) is not None:
            turn.append(("o", added_in(i), 0))
        if second(i, Y_GATE) is not None:
            turn.append(("g", second(i, Y_GATE), 0))
        if second(i, Y_T) is not None:
            turn.append(("y", second(i, Y_T), 0))
        if turned_in(i) is not None:
            turn += [("p", turned_in(i), k) for k in chunks(turned_in(i))]
    TURN_BANK, BEFORE, last_in = {}, {}, {}
    for n, item in enumerate(turn):
        at = RING + (n % TURNS if n < late else 1 + n % (TURNS - 1))
        TURN_BANK[item], BEFORE[item] = at, last_in.get(at)
        last_in[at] = item
    BEFORE["shared"] = last_in[RING]

    def on_act(c):
        return c % 2 == 0

    def act_turns(c):
        return sum(on_act(n) for n in range(c))

    def dve_turns(c):
        return c - act_turns(c)

    ROW_BU, ROW_BD = 0, SLOTS * FC
    ROW_GATE = ROW_BD + SLOTS
    ROWS = ROW_GATE + E
    assert ROWS <= P
    SA, CA, GA, SB, CB, GB = range(6)
    MOD_PART = [slice(0, 2), slice(2, 6)]

    w_dram = nc.dram_tensor("route_scratch", (NB, NT, E, P), F32, kind="Internal").ap()

    with ExitStack() as ctx:
        def sb(name, shape, dt=F32):
            return ctx.enter_context(nc.sbuf_tensor(name, shape, dt))

        def sem(name):
            return ctx.enter_context(nc.semaphore(name))

        bank = [ctx.enter_context(nc.psum_tensor(f"bank{i}", [P, BLOCK], F32)) for i in range(8)]

        ident = sb("ident", [P, P])
        ident_r = sb("ident_r", [P, P], F32R)
        mask = sb("mask", [P, P])
        mask_r = sb("mask_r", [P, P], F32R)
        rows = sb("rows", [P, P])
        cols = sb("cols", [P, ROWS])
        gate_b = sb("gate_b", [P, E])
        down_count = sb("down_count", [P, E])
        silu = sb("silu", [P, 4, NB])
        c_rows = sb("c_rows", [NB, P])
        mods = sb("mods", [P, 6 * NB])
        bias_now = sb("bias_now", [P, 2, FC])
        gsign = sb("gsign", [P, 2, NB])
        wqkv_hi = sb("wqkv_hi", [P, 3 * P], F32R)
        wqkv_lo = sb("wqkv_lo", [P, 3 * P], F32R)
        x_sb = sb("x_sb", [P, TILES * P])
        ln_const = sb("ln_const", [P, 4, TPB])
        EPS, MINUS_HALF, THREE_HALVES = range(3)
        stats = sb("stats", [P, 3, TPB, 6])
        moments = sb("moments", [P, 3, TPB, 2])
        ln_work = sb("ln_work", [P, 3, 4, TPB])
        rstd = sb("rstd", [P, 3, TPB])
        xn = sb("xn", [P, 2, BLOCK])
        xn2 = sb("xn2", [P, BLOCK])
        hT = sb("hT", [P, 2, BLOCK])
        hT_hi = sb("hT_hi", [P, 2, BLOCK], F32R)
        hT_lo = sb("hT_lo", [P, 2, BLOCK], F32R)
        h2T = sb("h2T", [P, BLOCK])
        h2_hi = sb("h2_hi", [P, TILES * P], F32R)
        h2_lo = sb("h2_lo", [P, TILES * P], F32R)
        kq_hi = sb("kq_hi", [P, TILES * P + QRING * BLOCK], F32R)
        kq_lo = sb("kq_lo", [P, TILES * P + QRING * BLOCK], F32R)
        v_sb = sb("v_sb", [P, SEQ])
        probs = sb("probs", [P, 2, SEQ])
        probsT = sb("probsT", [P, 2, NT * PAIR])
        chunk_max = sb("chunk_max", [P, 2, NQ])
        neg_max = sb("neg_max", [P, TILES])
        exp_sum = sb("exp_sum", [P, TILES, NQ])
        row_sum = sb("row_sum", [P, 2])
        row_inv = sb("row_inv", [P, 2])
        oT = sb("oT", [P, 2, PAIR])
        raw = sb("raw", [P, 2, 2, F])
        up_hi = sb("up_hi", [P, 2, F], F32R)
        up_lo = sb("up_lo", [P, 2, F], F32R)
        down_hi = sb("down_hi", [P, 2, FC * P], F32R)
        down_lo = sb("down_lo", [P, 2, FC * P], F32R)
        logits = sb("logits", [P, TILES * E])

        mod_raw = [bank[RING - 1][:, 0:6 * NB], bank[7][:, 0:6 * NB]]
        wmod_sb = probs[:, 0, 0:6 * P]
        wqkv = probs[:, 1, 0:3 * P]
        a_sb = probs[:, :, :]
        a_hi = kq_hi[:, 0:2 * FC * BLOCK].rearrange("p (u f) -> p u f", u=2)
        a_lo = kq_lo[:, 0:2 * FC * BLOCK].rearrange("p (u f) -> p u f", u=2)
        raw_up, raw_down = raw[:, 0, :, :], raw[:, 1, :, :]
        v_of = [v_sb[:, :], raw[:, :, :, :].rearrange("p j s f -> p (j s f)")]
        PCH = 2 * SEQ // BLOCK
        probs_at = probs[:, :, :].rearrange("p u (c k) -> p (u c) k", k=BLOCK)
        assert SEQ == FC * BLOCK and NT * PAIR == TILES * P and NB == 2
        acc = probsT[:, 0, :]
        w_bc = probsT[:, 1, :].rearrange("p (b t) -> p b t", b=NB)
        yw = xn
        accg = hT
        work = [v_sb[:, n * TILES * E:(n + 1) * TILES * E] for n in range(7)]
        score, tie, pick1, pick2 = (w.rearrange("p (n e) -> p n e", e=E) for w in work[0:4])
        weight = work[4]
        weightT = work[5].rearrange("p (b t) -> p b t", b=NB)
        best = work[6][:, 0:4 * TILES].rearrange("p (k n) -> p k n", k=4)

        x_in = [sem(f"x_in{n}") for n in range(NBLK)]
        c_in, c_T, biases_ready = sem("c_in"), sem("c_T"), sem("biases_ready")
        rows_in, qkv_in, gate_b_in = sem("rows_in"), sem("qkv_in"), sem("gate_b_in")
        wmod_in = [sem("wmod_in0"), sem("wmod_in1")]
        raw_in = [sem("raw_in0"), sem("raw_in1")]
        pool_ready = sem("pool_ready")
        consts_r = sem("consts_r")
        rows_T, cols_ready = sem("rows_T"), sem("cols_ready")
        silu_exp, silu_ready, mod_mm, mods_ready = sem("silu_exp"), sem("silu_ready"), sem("mod_mm"), sem("mods_ready")
        dve_step = sem("dve_step")
        moments_ready, rstd_ready = sem("moments_ready"), sem("rstd_ready")
        pool_step = sem("pool_step")
        xn_ready, xT_done = sem("xn_ready"), sem("xT_done")
        h_hi_done, h_lo_done = sem("h_hi_done"), sem("h_lo_done")
        qk_done, v_mm, qk_hi_done, qk_lo_done, v_done = sem("qk_done"), sem("v_mm"), sem("qk_hi_done"), sem("qk_lo_done"), sem("v_done")
        score_done, neg_max_ready, exp_done = sem("score_done"), sem("neg_max_ready"), sem("exp_done")
        pT_done, pT_act, pT_dve = sem("pT_done"), sem("pT_act"), sem("pT_dve")
        pv_done, oT_ready, oTT_done, x1_done = sem("pv_done"), sem("oT_ready"), sem("oTT_done"), sem("x1_done")
        x2n_ready, x2T_done, h2T_ready = sem("x2n_ready"), sem("x2T_done"), sem("h2T_ready")
        h2_lo_done, gate_done, logit_done = sem("h2_lo_done"), sem("gate_done"), sem("logit_done")
        sig_exp, weight_ready, weightT_mm, weightT_ready, weight_out = sem("sig_exp"), sem("weight_ready"), sem("weightT_mm"), sem("weightT_ready"), sem("weight_out")
        w_bc_in = [sem("w_bc_in0"), sem("w_bc_in1")]
        wT_done, w_hi_done, w_lo_done = sem("wT_done"), sem("w_hi_done"), sem("w_lo_done")
        a_hi_act = sem("a_hi_act")
        up_done, gelu_done, a_hi_done, a_lo_done = sem("up_done"), sem("gelu_done"), sem("a_hi_done"), sem("a_lo_done")
        START = 1
        down_done, yw_ready, acc_done = sem("down_done"), sem("yw_ready"), sem("acc_done")
        accg_ready, accT_done, out_ready, stored = sem("accg_ready"), sem("accT_done"), sem("out_ready"), sem("stored")

        x_tiles = x.rearrange("b (n p) d -> p b n d", p=P)
        out_tiles = out.rearrange("b (n p) d -> p b n d", p=P)
        x_view = x_sb[:, :].rearrange("p (b n d) -> p b n d", b=NB, n=NT)

        def tok(tile, n=1):
            return bass.ds(tile * P, n * P)

        def k_cols(n):
            return slice(n * BLOCK, (n + 1) * BLOCK)

        def q_cols(n, tile=0, tiles=TPB):
            at = TILES * P + n % QRING * BLOCK + tile * P
            return slice(at, at + tiles * P)

        def mod(j, b):
            return mods[:, j * NB + b:j * NB + b + 1]

        def route_cols(part):
            return slice(ROUTE_TILES[part].start * E, ROUTE_TILES[part].stop * E)

        def turn_bank(kind, i, k=0):
            return bank[TURN_BANK[kind, i, k]]

        def wmod_part(part):
            return slice(MOD_PART[part].start * P, MOD_PART[part].stop * P)

        block = ctx.enter_context(nc.Block())

        @block.sync
        def _(sync):
            def load_raw(s, up, down):
                sync.dma_start(raw_up[:, s % 2, :].rearrange("p (f h) -> p f h", f=FC),
                               up.rearrange("(f p) h -> p f h", p=P)).then_inc(raw_in[s % 2], 16)
                sync.dma_start(raw_down[:, s % 2, :], down).then_inc(raw_in[s % 2], 16)

            def load_x(n):
                b, q = divmod(n, NQ)
                at = slice(q * TPB, (q + 1) * TPB)
                sync.dma_start(x_view[:, b, at, :], x_tiles[:, b, at, :]).then_inc(x_in[n], 16)

            load_x(0)
            load_raw(0, sWu, sWd)
            load_x(1)
            for at, src in ((ROW_BU, sbu.rearrange("(c f) -> c f", f=P)),
                            (ROW_BU + FC, bu.rearrange("e (c f) -> (e c) f", f=P)),
                            (ROW_BD, sbd.rearrange("(o h) -> o h", o=1)),
                            (ROW_BD + 1, bd), (ROW_GATE, gate_w)):
                sync.dma_start(rows[at:at + src.shape[0], :], src).then_inc(rows_in, 16)
            sync.dma_start(wmod_sb[:, wmod_part(1)], wmod[:, wmod_part(1)]).then_inc(wmod_in[1], 16)
            load_x(2)
            load_raw(1, Wu[0], Wd[0])
            sync.dma_start(gate_b[:, :], gate_bias.rearrange("(o e) -> o e", o=1).broadcast_to([P, E])
                           ).then_inc(gate_b_in, 16)
            for n in range(3, NBLK):
                load_x(n)
            sync.wait_ge(pv_done, PAIRS)
            for s in (2, 3):
                load_raw(s, Wu[s - 1], Wd[s - 1])

            sync.wait_ge(weightT_ready, NB)
            sync.dma_start(w_dram.rearrange("b n e t -> (n e) b t"), weightT[:, :, :]).then_inc(weight_out, 16)
            sync.wait_ge(weight_out, 16)

            def load_weights_bc(s, e, b):
                sync.dma_start(w_bc[:, b, :].rearrange("p (n t) -> p n t", n=NT),
                               w_dram[b, :, e, :].rearrange("n (o t) -> o n t", o=1).broadcast_to([P, NT, P])
                               ).then_inc(w_bc_in[b], 16)

            for b in range(NB):
                load_weights_bc(1, 0, b)
            for s in range(2, SLOTS):
                if s + 2 < SLOTS:
                    sync.wait_ge(wT_done, 2 * s + 2)
                    load_raw(s + 2, Wu[s + 1], Wd[s + 1])
                for b in range(NB):
                    sync.wait_ge(yw_ready, START + NBLK * (s - 1) + NQ * (b + 1))
                    load_weights_bc(s, s - 1, b)

            for n in range(NBLK):
                b, q = n // NQ, n % NQ
                sync.wait_ge(out_ready, n + 1)
                sync.dma_start(out_tiles[:, b, TPB * q:TPB * (q + 1), :],
                               x_view[:, b, TPB * q:TPB * (q + 1), :]).then_inc(stored, 16)
            sync.wait_ge(stored, 16 * NBLK)

        @block.gpsimd
        def _(pool):
            pool.sem_inc(acc_done, START)
            nc.gpsimd.memset(ident[:, :], 0.0).then_inc(pool_ready, 1)
            for n, value in ((EPS, LN_EPS), (MINUS_HALF, -0.5), (THREE_HALVES, 1.5)):
                last = nc.gpsimd.memset(ln_const[:, n, :], value)
            last.then_inc(pool_ready, 1)
            nc.gpsimd.memset(mask[:, :], 0.0).then_inc(pool_ready, 1)
            nc.gpsimd.iota(down_count[:, :], pattern=[[-1, E]], base=E, channel_multiplier=0,
                           allow_small_or_imprecise_dtypes=True).then_inc(pool_ready, 1)
            pool.wait_ge(pool_ready, 4)
            nc.gpsimd.affine_select(out=ident[:, :], in_=ident[:, :], compare_op=ALU.not_equal, fill=1.0, base=0,
                                    pattern=[[-1, P]], channel_multiplier=1).then_inc(pool_ready, 1)
            nc.gpsimd.affine_select(out=mask[:, :], in_=mask[:, :], compare_op=ALU.is_ge, fill=MASKED, base=0,
                                    pattern=[[-1, P]], channel_multiplier=1).then_inc(pool_ready, 1)

            own = Steps()

            def inverse_std(norm):
                at = norm_place(norm)
                tt, k, var, r = nc.gpsimd.tensor_tensor, ln_const, moments[:, at, :, 1], rstd[:, at, :]
                v, guess, h, w = (ln_work[:, at, n, :] for n in range(4))
                pool.wait_ge(moments_ready, norm_count(norm))
                tt(v, var, k[:, EPS, :], ALU.add).then_inc(pool_step, 1)
                pool.wait_ge(pool_step, own.next())
                tt(guess, v, k[:, MINUS_HALF, :], ALU.pow)
                tt(h, v, k[:, MINUS_HALF, :], ALU.mult).then_inc(pool_step, 1)
                pool.wait_ge(pool_step, own.next())
                tt(w, guess, guess, ALU.mult).then_inc(pool_step, 1)
                pool.wait_ge(pool_step, own.next())
                tt(w, w, h, ALU.mult).then_inc(pool_step, 1)
                pool.wait_ge(pool_step, own.next())
                tt(w, w, k[:, THREE_HALVES, :], ALU.add).then_inc(pool_step, 1)
                pool.wait_ge(pool_step, own.next())
                tt(r, w, guess, ALU.mult).then_inc(rstd_ready, 1)

            def h2_low(n):
                at = tok(n * TPB, TPB)
                pool.wait_ge(h2T_ready, n + 1)
                nc.gpsimd.tensor_tensor(h2_lo[:, at], h2T[:, :], h2_hi[:, at].bitcast(F32),
                                        ALU.subtract).then_inc(h2_lo_done, 1)

            for i in range(FIRST_STEP, STEPS):
                if phase(i, X_STATS) is not None:
                    inverse_std(("x", phase(i, X_STATS)))
                if second(i, Y_STATS) is not None:
                    inverse_std(("y", second(i, Y_STATS)))
                if second(i, Y_T) is not None:
                    h2_low(second(i, Y_T))

            with pool.Fori(1, SLOTS) as s:
                with pool.Fori(0, NQ) as half:
                    for par in range(2):
                        u = s * NBLK + half * 2 + par
                        at = bass.ds(half * (2 * BLOCK) + par * BLOCK, BLOCK)
                        pool.wait_ge(yw_ready, START + u + 1)
                        pool.wait_ge(acc_done, START + u - NBLK)
                        nc.gpsimd.tensor_tensor(acc[:, at], acc[:, at], yw[:, par, :], ALU.add).then_inc(acc_done, 1)

        @block.tensor
        def _(pe):
            def transposes(dst, src, n=TPB):
                for t in range(n):
                    last = nc.tensor.transpose(dst[:, t * P:(t + 1) * P], src[:, t * P:(t + 1) * P], ident[:, :])
                return last

            def three(dst, w_hi, w_lo, m_hi, m_lo, start, stop):
                nc.tensor.matmul(dst, w_hi, m_hi, start=start, stop=False)
                nc.tensor.matmul(dst, w_hi, m_lo, start=False, stop=False)
                return nc.tensor.matmul(dst, w_lo, m_hi, start=False, stop=stop)

            def weights_T(s, loads, dst=lambda j: bank[5 + j]):
                pe.wait_ge(raw_in[s % 2], 32 * loads)
                for j, src in ((0, raw_up), (1, raw_down)):
                    transposes(dst(j), src[:, s % 2, :], FC).then_inc(wT_done, 1)

            def rows_to_columns():
                pe.wait_ge(pool_ready, 6)
                pe.wait_ge(rows_in, 16 * 5)
                nc.tensor.transpose(bank[6][:, 0:ROWS], rows[0:ROWS, :], ident[0:ROWS, 0:ROWS]).then_inc(rows_T, 1)

            def modulation(part):
                pe.wait_ge(silu_ready, 1)
                pe.wait_ge(wmod_in[part], 16)
                for j in range(6)[MOD_PART[part]]:
                    last = nc.tensor.matmul(mod_raw[part][:, j * NB:(j + 1) * NB], wmod_sb[:, j * P:(j + 1) * P],
                                            silu[:, 3, :], start=True, stop=True)
                last.then_inc(mod_mm, 1)

            def wait_turn(item):
                if BEFORE[item]:
                    kind, i, k = BEFORE[item]
                    if kind == "x":
                        pe.wait_ge(h_hi_done, i + 1)
                    elif kind == "o":
                        pe.wait_ge(x1_done, i + 1)
                    elif kind == "y":
                        pe.wait_ge(h2T_ready, i + 1)
                    elif kind == "g":
                        pe.wait_ge(logit_done, i + 1)
                    elif on_act(CHUNK[i] + k):
                        pe.wait_ge(pT_act, act_turns(CHUNK[i] + k) + 1)
                    else:
                        pe.wait_ge(pT_dve, dve_turns(CHUNK[i] + k) + 1)

            def into(item):
                wait_turn(item)
                return turn_bank(*item)

            def wait_ring(item):
                n = SLOT[item]
                if n >= RING:
                    kind, i, k = ring[n - RING]
                    if kind == "v":
                        pe.wait_ge(v_done, i + 1)
                    elif kind == "s":
                        pe.wait_ge(exp_done, CHUNK[i] + k + 1)
                    elif kind == "w":
                        pe.wait_ge(w_lo_done, 2 * i + k + 1)
                    else:
                        pe.wait_ge(qk_lo_done, 2 * i + (kind == "k") + 1)
                return bank[n % RING]

            def x_T(n):
                pe.wait_ge(xn_ready, n + 1)
                if n == 1:
                    pe.wait_ge(cols_ready, 1)
                transposes(into(("x", n, 0)), xn[:, n % 2, :]).then_inc(xT_done, 1)

            def project_qk(n):
                pe.wait_ge(h_lo_done, n + 1)
                if n == 0:
                    pe.wait_ge(consts_r, 3)
                for j in range(2):
                    w = slice(j * P, (j + 1) * P)
                    three(wait_ring(("qk"[j], n, 0))[:, :], wqkv_hi[:, w], wqkv_lo[:, w], hT_hi[:, n % 2, :],
                          hT_lo[:, n % 2, :], True, True).then_inc(qk_done, 1)

            def project_v(n):
                w = slice(2 * P, 3 * P)
                dst = wait_ring(("v", n, 0))
                for t in range(TPB):
                    ts = slice(t * P, (t + 1) * P)
                    last = three(dst[:, ts], hT_hi[:, n % 2, ts], hT_lo[:, n % 2, ts], wqkv_hi[:, w],
                                 wqkv_lo[:, w], True, True)
                last.then_inc(v_mm, 1)

            def scores(i):
                b, t = divmod(i, NT)
                n = i // TPB
                pe.wait_ge(qk_lo_done, 2 * n + 2)
                q_at = q_cols(n, t % TPB, 1)
                for k in chunks(i):
                    n = key_tiles(i, k) * P
                    dst = wait_ring(("s", i, k))
                    k_at = slice(b * SEQ + k * BLOCK, b * SEQ + k * BLOCK + n)
                    nc.tensor.matmul(dst[:, 0:n], kq_hi[:, q_at], kq_hi[:, k_at], start=True, stop=False)
                    if k == t // TPB:
                        nc.tensor.matmul(dst[:, n - P:n], ident_r[:, :], mask_r[:, :], start=False, stop=False)
                    nc.tensor.matmul(dst[:, 0:n], kq_hi[:, q_at], kq_lo[:, k_at], start=False, stop=False)
                    nc.tensor.matmul(dst[:, 0:n], kq_lo[:, q_at], kq_hi[:, k_at], start=False,
                                     stop=True).then_inc(score_done, 1)

            def probs_T(i):
                for k in chunks(i):
                    dst = into(("p", i, k))
                    pe.wait_ge(exp_done, CHUNK[i] + k + 1)
                    transposes(dst, probs_at[:, (CHUNK[i] + k) % PCH, :], key_tiles(i, k)).then_inc(pT_done, 1)

            def pv(r, half):
                b, p = divmod(r, NT // 2)
                if half == 0:
                    pe.wait_ge(v_done, r // 2 + 1)
                    if r:
                        pe.wait_ge(oT_ready, r)
                    else:
                        pe.wait_ge(mods_ready, 2)
                    pe.wait_ge(pT_act, act_turns(CHUNK[2 * r + 2]))
                    pe.wait_ge(pT_dve, dve_turns(CHUNK[2 * r + 2]))
                for j in range(half * (p + 1), (half + 1) * (p + 1)):
                    lo = P if j == 2 * p + 1 else 0
                    mm = nc.tensor.matmul(bank[7][:, lo:PAIR], v_of[b][:, j * P:(j + 1) * P],
                                          probsT[:, r % 2, j * PAIR + lo:(j + 1) * PAIR], start=(j == 0),
                                          stop=(j == 2 * p + 1))
                if half:
                    mm.then_inc(pv_done, 1)

            def o_T(r):
                dst = into(("o", r, 0))
                pe.wait_ge(oT_ready, r + 1)
                transposes(dst, oT[:, r % 2, :], 2).then_inc(oTT_done, 1)

            def x2_T(n):
                dst = into(("y", n, 0))
                pe.wait_ge(x2n_ready, n + 1)
                transposes(dst, xn2[:, :]).then_inc(x2T_done, 1)

            def gate(n):
                dst = into(("g", n, 0))
                pe.wait_ge(h2T_ready, n + 1)
                for t in range(TPB):
                    last = nc.tensor.matmul(dst[:, t * E:(t + 1) * E], h2T[:, t * P:(t + 1) * P],
                                            cols[:, ROW_GATE:ROW_GATE + E], start=True, stop=True)
                last.then_inc(gate_done, 1)

            def up(s, u, blk, at):
                for f in range(FC):
                    fs = slice(f * P, (f + 1) * P)
                    if not (isinstance(u, int) and u < 1):
                        pe.wait_ge(gelu_done, FC * u - FC + f + 1)
                    three(bank[f][:, :], up_hi[:, s % 2, fs], up_lo[:, s % 2, fs], h2_hi[:, bass.ds(at, BLOCK)],
                          h2_lo[:, bass.ds(at, BLOCK)], True, True).then_inc(up_done, 1)

            def down(s, u, par):
                if not (isinstance(u, int) and u < 2):
                    pe.wait_ge(yw_ready, START + u - 1)
                for f in range(FC):
                    if f % 2 == 0:
                        pe.wait_ge(a_lo_done, 2 * u + f // 2 + 1)
                    fs, at = slice(f * P, (f + 1) * P), slice(f * BLOCK, (f + 1) * BLOCK)
                    mm = three(bank[Y_BANK[par]][:, :], down_hi[:, s % 2, fs], down_lo[:, s % 2, fs],
                               a_hi[:, par, at], a_lo[:, par, at], f == 0, f == FC - 1)
                mm.then_inc(down_done, 1)

            def slot(s, base, n_slot, loads, prefetch):
                pe.wait_ge(w_lo_done, 2 * n_slot + 2)
                up(s, base, 0, 0)
                down(s + 1, base - 1, 1)
                up(s, base + 1, 1, BLOCK)
                down(s, base, 0)
                if prefetch:
                    pe.wait_ge(weightT_ready, NB)
                    weights_T(s + 1, loads)
                with pe.Fori(1, NBLK // 2) as it:
                    up(s, base + it * 2, 0, it * (2 * BLOCK))
                    down(s, base + it * 2 - 1, 1)
                    up(s, base + it * 2 + 1, 1, it * (2 * BLOCK) + BLOCK)
                    down(s, base + it * 2, 0)

            def shared_unit(n):
                if n == 0:
                    pe.wait_ge(w_lo_done, 2)
                if n == 1:
                    wait_turn("shared")
                pe.wait_ge(h2_lo_done, n + 1)
                up(0, n, n % 2, n * BLOCK)
                if n == NBLK - 1:
                    pe.wait_ge(weight_ready, ROUTES)
                    for b in range(NB):
                        last = nc.tensor.transpose(bank[6][:, b * P:(b + 1) * P],
                                                   weight[:, b * NT * E:(b + 1) * NT * E], ident[:, :])
                    last.then_inc(weightT_mm, 1)
                if n > 0:
                    down(0, n - 1, (n - 1) % 2)

            for i in range(FIRST_STEP, STEPS):
                if i == FIRST_STEP:
                    pe.wait_ge(pool_ready, 6)
                    pe.wait_ge(c_in, 16)
                    nc.tensor.transpose(bank[2][:, 0:NB], c_rows[:, :], ident[0:NB, 0:NB]).then_inc(c_T, 1)
                    modulation(0)
                if phase(i, X_T) is not None:
                    x_T(phase(i, X_T))
                if phase(i, X_QK) is not None:
                    project_qk(phase(i, X_QK))
                if phase(i, X_V) is not None:
                    project_v(phase(i, X_V))
                if 0 <= i < TILES:
                    scores(i)
                if added_in(i) is not None:
                    o_T(added_in(i))
                if second(i, Y_GATE) is not None:
                    gate(second(i, Y_GATE))
                if second(i, Y_T) is not None:
                    x2_T(second(i, Y_T))
                if pv_of(i):
                    pv(*pv_of(i))
                if turned_in(i) is not None:
                    probs_T(turned_in(i))
                if i == STARTS[0] + X_QK:
                    rows_to_columns()
                    modulation(1)
                if weights_in(i) is not None:
                    weights_T(weights_in(i), 1, lambda j: wait_ring(("w", weights_in(i), j)))
                if i in SHARED_AT:
                    shared_unit(SHARED_AT.index(i))

            pe.wait_ge(logit_done, NBLK)
            for n in range(len(SHARED_AT), NBLK):
                shared_unit(n)
            with pe.Fori(0, (SLOTS - 3) // 2) as pair:
                for par in (1, 2):
                    n = pair * 2 + par
                    slot(par, n * NBLK, n, pair + 2, True)
            slot(SLOTS - 2, (SLOTS - 2) * NBLK, SLOTS - 2, (SLOTS - 1) // 2 + 1, True)

            def sum_T(n):
                pe.wait_ge(accg_ready, n + 1)
                if n >= 2:
                    pe.wait_ge(out_ready, n - 1)
                transposes(bank[5 + n % 2], accg[:, n % 2, :]).then_inc(accT_done, 1)

            base = (SLOTS - 1) * NBLK
            pe.wait_ge(w_lo_done, 2 * SLOTS)
            for n in range(NBLK):
                up(SLOTS - 1, base + n, n % 2, n * BLOCK)
                down(SLOTS - 1 if n else SLOTS - 2, base + n - 1, (n - 1) % 2)
                if n >= SUM_LAG:
                    sum_T(n - SUM_LAG)
            down(SLOTS - 1, base + NBLK - 1, 1)
            for n in range(NBLK - SUM_LAG, NBLK):
                sum_T(n)

        @block.scalar
        def _(act):
            act.dma_start(c_rows[:, :], c).then_inc(c_in, 16)
            act.dma_start(wmod_sb[:, wmod_part(0)], wmod[:, wmod_part(0)]).then_inc(wmod_in[0], 16)
            act.dma_start(wqkv[:, 0:P], Wq).then_inc(qkv_in, 16)

            def weights_hi(s, n_slot, src=lambda j: bank[5 + j]):
                for j, dst in ((0, up_hi), (1, down_hi)):
                    act.wait_ge(wT_done, 2 * n_slot + j + 1)
                    nc.scalar.copy(dst[:, s % 2, :], src(j)[:, :]).then_inc(w_hi_done, 1)

            act.wait_ge(c_T, 1)
            nc.scalar.activation(silu[:, 0, :], bank[2][:, 0:NB], ACT.Exp, scale=-1.0).then_inc(silu_exp, 1)
            act.dma_start(wqkv[:, P:2 * P], Wk).then_inc(qkv_in, 16)
            act.dma_start(wqkv[:, 2 * P:3 * P], Wv).then_inc(qkv_in, 16)

            def h_hi(n):
                b = n // NQ
                act.wait_ge(xT_done, n + 1)
                if n >= 2:
                    act.wait_ge(h_lo_done, n - 1)
                    act.wait_ge(v_mm, n - 1)
                if n == 0:
                    act.wait_ge(mods_ready, 1)
                src = turn_bank("x", n)
                nc.scalar.activation(hT[:, n % 2, :], src[:, :], ACT.Identity, bias=mod(SA, b), scale=mod(CA, b))
                nc.scalar.activation(hT_hi[:, n % 2, :], src[:, :], ACT.Identity, bias=mod(SA, b),
                                     scale=mod(CA, b)).then_inc(h_hi_done, 1)

            def qk_high(n):
                act.wait_ge(qk_done, 2 * n + 1)
                if n >= QRING:
                    act.wait_ge(score_done, CHUNK[(n - QRING + 1) * TPB])
                nc.scalar.activation(kq_hi[:, q_cols(n)], bank[SLOT["q", n, 0] % RING][:, :], ACT.Copy,
                                     scale=SCALE).then_inc(qk_hi_done, 1)
                act.wait_ge(qk_done, 2 * n + 2)
                nc.scalar.copy(kq_hi[:, k_cols(n)], bank[SLOT["k", n, 0] % RING][:, :]).then_inc(qk_hi_done, 1)

            def v_out(n):
                b, q = divmod(n, NQ)
                act.wait_ge(v_mm, n + 1)
                nc.scalar.copy(v_of[b][:, q * BLOCK:(q + 1) * BLOCK],
                               bank[SLOT["v", n, 0] % RING][:, :]).then_inc(v_done, 1)

            def exps(i, k):
                c = CHUNK[i] + k
                if k == 0:
                    act.wait_ge(neg_max_ready, i + 1)
                if c >= PCH:
                    act.wait_ge(pT_done, c - PCH + 1)
                n = key_tiles(i, k) * P
                nc.scalar.activation(probs_at[:, c % PCH, 0:n], bank[SLOT["s", i, k] % RING][:, 0:n], ACT.Exp,
                                     bias=neg_max[:, i:i + 1],
                                     accum_out=exp_sum[:, i, k:k + 1]).then_inc(exp_done, 1)

            def probs_out(i, k):
                c = CHUNK[i] + k
                act.wait_ge(pT_done, c + 1)
                if i >= 4:
                    act.wait_ge(pv_done, i // 2 - 1)
                n = key_tiles(i, k)
                at = i % 2 * P
                dst = probsT[:, i // 2 % 2, :].rearrange("p (j t) -> p j t", t=PAIR)
                src = turn_bank("p", i, k)[:, 0:n * P].rearrange("p (j t) -> p j t", t=P)
                nc.scalar.copy(dst[:, TPB * k:TPB * k + n, at:at + P], src).then_inc(pT_act, 1)

            def o_out(r):
                act.wait_ge(pv_done, r + 1)
                if r == 0:
                    act.wait_ge(mods_ready, 2)
                if r >= 2:
                    act.wait_ge(oTT_done, r - 1)
                nc.scalar.activation(oT[:, r % 2, :], bank[7][:, 0:PAIR], ACT.Copy,
                                     scale=mod(GA, r // (NT // 2))).then_inc(oT_ready, 1)

            def h2(n):
                b = n // NQ
                act.wait_ge(x2T_done, n + 1)
                if n >= 1:
                    act.wait_ge(gate_done, n)
                    act.wait_ge(h2_lo_done, n)
                src = turn_bank("y", n)
                nc.scalar.activation(h2T[:, :], src[:, :], ACT.Identity, bias=mod(SB, b), scale=mod(CB, b))
                nc.scalar.activation(h2_hi[:, tok(n * TPB, TPB)], src[:, :], ACT.Identity,
                                     bias=mod(SB, b), scale=mod(CB, b)).then_inc(h2T_ready, 1)

            def gelus(s, u, par):
                for f in range(FC):
                    act.wait_ge(up_done, FC * u + f + 1)
                    if f % 2 == 0 and not (isinstance(u, int) and u < 2):
                        act.wait_ge(a_lo_done, 2 * u + f // 2 - 3)
                    nc.scalar.activation(a_sb[:, par, f * BLOCK:(f + 1) * BLOCK], bank[f][:, :], ACT.Gelu,
                                         bias=bias_now[:, s % 2, f:f + 1]).then_inc(gelu_done, 1)

            def shared_unit(n):
                if n == 0:
                    act.wait_ge(biases_ready, 1)
                gelus(0, n, n % 2)
                if n >= 2:
                    act.wait_ge(down_done, n - 1)
                act.wait_ge(gelu_done, FC * (n + 1))
                at = slice(FC // 2 * BLOCK, FC * BLOCK)
                nc.scalar.copy(a_hi[:, n % 2, at], a_sb[:, n % 2, at]).then_inc(a_hi_act, 1)

            def sigmoid_exp(part):
                at = route_cols(part)
                act.wait_ge(logit_done, at.stop // (TPB * E))
                nc.scalar.activation(work[0][:, at], logits[:, at], ACT.Exp, scale=-1.0).then_inc(sig_exp, 1)

            for i in range(FIRST_STEP, STEPS):
                if phase(i, X_T) is not None:
                    h_hi(phase(i, X_T))
                if phase(i, X_QK) is not None:
                    qk_high(phase(i, X_QK))
                if phase(i, X_V) is not None:
                    v_out(phase(i, X_V))
                if added_in(i) is not None:
                    o_out(added_in(i))
                if second(i, Y_T) is not None:
                    h2(second(i, Y_T))
                t = turned_in(i)
                for k in range(NQ + EXP_LEAD):
                    if 0 <= i < TILES and k in chunks(i):
                        exps(i, k)
                    if t is not None and k - EXP_LEAD in chunks(t) and on_act(CHUNK[t] + k - EXP_LEAD):
                        probs_out(t, k - EXP_LEAD)
                s = weights_in(i)
                if s is not None:
                    weights_hi(s, s, lambda j: bank[SLOT["w", s, j] % RING])
                if i == ROUTE_AT:
                    sigmoid_exp(0)
                if i in SHARED_AT:
                    shared_unit(SHARED_AT.index(i))

            sigmoid_exp(1)
            for n in range(len(SHARED_AT), NBLK):
                shared_unit(n)

            def slot(s, base, n_slot, prefetch):
                act.wait_ge(w_lo_done, 2 * n_slot + 2)
                gelus(s, base, 0)
                gelus(s, base + 1, 1)
                if prefetch:
                    act.wait_ge(down_done, base)
                    weights_hi(s + 1, n_slot + 1)
                with act.Fori(1, NBLK // 2) as it:
                    for par in range(2):
                        gelus(s, base + it * 2 + par, par)

            with act.Fori(0, (SLOTS - 3) // 2) as pair:
                for par in (1, 2):
                    slot(par, (pair * 2 + par) * NBLK, pair * 2 + par, True)
            slot(SLOTS - 2, (SLOTS - 2) * NBLK, SLOTS - 2, True)

            def scale_sum(n):
                act.wait_ge(acc_done, START + (SLOTS - 2) * NBLK + n + 1)
                if n >= 2:
                    act.wait_ge(accT_done, n - 1)
                nc.scalar.activation(accg[:, n % 2, :], acc[:, n * BLOCK:(n + 1) * BLOCK], ACT.Copy,
                                     scale=mod(GB, n // NQ)).then_inc(accg_ready, 1)

            act.wait_ge(w_lo_done, 2 * SLOTS)
            for n in range(NBLK):
                gelus(SLOTS - 1, (SLOTS - 1) * NBLK + n, n % 2)
                if n >= SUM_LAG:
                    scale_sum(n - SUM_LAG)
            for n in range(NBLK - SUM_LAG, NBLK):
                scale_sum(n)

        @block.vector
        def _(dve):
            dve.sem_inc(yw_ready, START)

            def weights_lo(s, n_slot, src=lambda j: bank[5 + j]):
                if not isinstance(n_slot, int) or n_slot > 1:
                    nc.vector.tensor_copy(bias_now[:, s % 2, :], cols[:, bass.ds(n_slot * FC + ROW_BU, FC)])
                for j, hi, lo in ((0, up_hi, up_lo), (1, down_hi, down_lo)):
                    dve.wait_ge(w_hi_done, 2 * n_slot + j + 1)
                    nc.vector.tensor_tensor(lo[:, s % 2, :], src(j)[:, :], hi[:, s % 2, :].bitcast(F32),
                                            ALU.subtract).then_inc(w_lo_done, 1)

            step = Steps()

            dve.wait_ge(pool_ready, 6)
            nc.vector.tensor_copy(ident_r[:, :], ident[:, :]).then_inc(consts_r, 1)
            nc.vector.tensor_copy(mask_r[:, :], mask[:, :])

            def silu_of_c():
                dve.wait_ge(silu_exp, 1)
                nc.vector.tensor_scalar(silu[:, 1, :], silu[:, 0, :], 1.0, None, ALU.add).then_inc(dve_step, 1)
                dve.wait_ge(dve_step, step.next())
                nc.vector.reciprocal(silu[:, 2, :], silu[:, 1, :]).then_inc(dve_step, 1)
                dve.wait_ge(dve_step, step.next())
                nc.vector.tensor_tensor(silu[:, 3, :], silu[:, 2, :], bank[2][:, 0:NB], ALU.mult).then_inc(silu_ready, 1)

            def columns():
                dve.wait_ge(rows_T, 1)
                nc.vector.tensor_copy(cols[:, :], bank[6][:, 0:ROWS]).then_inc(cols_ready, 1)
                dve.wait_ge(cols_ready, 1)
                nc.vector.tensor_copy(bias_now[:, :, :], cols[:, ROW_BU:ROW_BU + 2 * FC].rearrange("p (s f) -> p s f", s=2)
                                      ).then_inc(biases_ready, 1)

            def projection_weights():
                dve.wait_ge(qkv_in, 48)
                nc.vector.tensor_copy(wqkv_hi[:, :], wqkv[:, :]).then_inc(consts_r, 1)
                dve.wait_ge(consts_r, 2)
                nc.vector.tensor_tensor(wqkv_lo[:, :], wqkv[:, :], wqkv_hi[:, :].bitcast(F32), ALU.subtract).then_inc(consts_r, 1)

            def shift_and_scale(src, shift, scale):
                nc.vector.tensor_copy(mods[:, shift * NB:(shift + 1) * NB], src[:, shift * NB:(shift + 1) * NB])
                return nc.vector.tensor_scalar(mods[:, scale * NB:(scale + 1) * NB], src[:, scale * NB:(scale + 1) * NB],
                                               1.0, None, ALU.add)

            def first_mods():
                dve.wait_ge(mod_mm, 1)
                shift_and_scale(mod_raw[0], SA, CA).then_inc(mods_ready, 1)

            def other_mods():
                dve.wait_ge(mod_mm, 2)
                shift_and_scale(mod_raw[1], SB, CB)
                assert (GA, GB) == (2, 5)
                gates, raw_gates = (ap.rearrange("p (g j b) -> p g j b", g=2, b=NB)[:, :, GA, :] for ap in (mods[:, :], mod_raw[1]))
                nc.vector.tensor_scalar(gsign[:, :, :], raw_gates, 0.0, 2.0, ALU.is_ge, ALU.mult).then_inc(dve_step, 1)
                dve.wait_ge(dve_step, step.next())
                nc.vector.tensor_scalar(gsign[:, :, :], gsign[:, :, :], -1.0, None, ALU.add).then_inc(dve_step, 1)
                dve.wait_ge(dve_step, step.next())
                nc.vector.tensor_tensor(gates, gsign[:, :, :], raw_gates, ALU.mult).then_inc(dve_step, 1)
                dve.wait_ge(dve_step, step.next())
                nc.vector.scalar_tensor_tensor(out=gates, in0=gates, scalar=0.25, in1=gsign[:, :, :],
                                               op0=ALU.max, op1=ALU.mult).then_inc(mods_ready, 1)

            def signal(instruction):
                instruction.then_inc(dve_step, 1)
                return step.next()

            count_of = {}

            def take_statistics(norm):
                for t in range(TPB):
                    last = nc.vector.bn_stats(stats[:, norm_place(norm), t, :], x_sb[:, tok(norm[1] * TPB + t)])
                count_of["statistics", norm] = signal(last)

            def take_moments(norm):
                at = norm_place(norm)
                dve.wait_ge(dve_step, count_of["statistics", norm])
                for t in range(TPB):
                    last = nc.vector.bn_aggr(moments[:, at, t, :], stats[:, at, t, :])
                last.then_inc(moments_ready, 1)

            def normalise(dst, norm):
                at = norm_place(norm)
                dve.wait_ge(rstd_ready, norm_count(norm))
                for t in range(TPB):
                    last = nc.vector.tensor_scalar(dst[:, t * P:(t + 1) * P], x_sb[:, tok(norm[1] * TPB + t)],
                                                   moments[:, at, t, 0:1], rstd[:, at, t:t + 1],
                                                   ALU.subtract, ALU.mult)
                return last

            def x_statistics(n):
                dve.wait_ge(x_in[n], 16)
                take_statistics(("x", n))

            def x_norm(n):
                if n >= 2:
                    dve.wait_ge(xT_done, n - 1)
                normalise(xn[:, n % 2, :], ("x", n)).then_inc(xn_ready, 1)

            def h_low(n):
                dve.wait_ge(h_hi_done, n + 1)
                if n >= 2:
                    dve.wait_ge(v_mm, n - 1)
                nc.vector.tensor_tensor(hT_lo[:, n % 2, :], hT[:, n % 2, :], hT_hi[:, n % 2, :].bitcast(F32),
                                        ALU.subtract).then_inc(h_lo_done, 1)

            def qk_low(n):
                at = q_cols(n)
                dve.wait_ge(qk_hi_done, 2 * n + 1)
                nc.vector.scalar_tensor_tensor(out=kq_lo[:, at], in0=bank[SLOT["q", n, 0] % RING][:, :], scalar=SCALE,
                                               in1=kq_hi[:, at].bitcast(F32), op0=ALU.mult,
                                               op1=ALU.subtract).then_inc(qk_lo_done, 1)
                at = k_cols(n)
                dve.wait_ge(qk_hi_done, 2 * n + 2)
                nc.vector.tensor_tensor(kq_lo[:, at], bank[SLOT["k", n, 0] % RING][:, :],
                                        kq_hi[:, at].bitcast(F32), ALU.subtract).then_inc(qk_lo_done, 1)

            def row_max(i):
                many = len(chunks(i)) > 1
                for k in chunks(i):
                    n = key_tiles(i, k) * P
                    dve.wait_ge(score_done, CHUNK[i] + k + 1)
                    dst = chunk_max[:, i % 2, k:k + 1] if many else neg_max[:, i:i + 1]
                    last = nc.vector.tensor_reduce(dst, bank[SLOT["s", i, k] % RING][:, 0:n], AX_X, ALU.max,
                                                   negate=not many)
                if many:
                    dve.wait_ge(dve_step, signal(last))
                    last = nc.vector.tensor_reduce(neg_max[:, i:i + 1], chunk_max[:, i % 2, 0:len(chunks(i))], AX_X,
                                                   ALU.max, negate=True)
                last.then_inc(neg_max_ready, 1)

            def probs_out(i, k):
                c = CHUNK[i] + k
                dve.wait_ge(pT_done, c + 1)
                if i >= 4:
                    dve.wait_ge(pv_done, i // 2 - 1)
                n = key_tiles(i, k)
                at = i % 2 * P
                dst = probsT[:, i // 2 % 2, :].rearrange("p (j t) -> p j t", t=PAIR)
                src = turn_bank("p", i, k)[:, 0:n * P].rearrange("p (j t) -> p j t", t=P)
                nc.vector.tensor_copy(dst[:, TPB * k:TPB * k + n, at:at + P], src).then_inc(pT_dve, 1)

            def residual(r):
                dve.wait_ge(dve_step, count_of["row_inv", r])
                dve.wait_ge(oTT_done, r + 1)
                src = turn_bank("o", r)
                for t in range(2):
                    at = tok(2 * r + t)
                    last = nc.vector.scalar_tensor_tensor(out=x_sb[:, at], in0=src[:, t * P:(t + 1) * P],
                                                          scalar=row_inv[:, t:t + 1], in1=x_sb[:, at],
                                                          op0=ALU.mult, op1=ALU.add)
                last.then_inc(x1_done, 1)

            def x2_statistics(n):
                dve.wait_ge(x1_done, 2 * n + 2)
                take_statistics(("y", n))

            def x2_norm(n):
                if n >= 1:
                    dve.wait_ge(x2T_done, n)
                normalise(xn2[:, :], ("y", n)).then_inc(x2n_ready, 1)

            def logits_out(n):
                dve.wait_ge(gate_done, n + 1)
                if n == 0:
                    dve.wait_ge(gate_b_in, 16)
                at = slice(n * TPB * E, (n + 1) * TPB * E)
                nc.vector.tensor_tensor(logits[:, at].rearrange("p (n e) -> p n e", e=E),
                                        turn_bank("g", n)[:, 0:TPB * E].rearrange("p (n e) -> p n e", e=E),
                                        gate_b[:, :].rearrange("p (o e) -> p o e", o=1).broadcast_to([P, TPB, E]),
                                        ALU.add).then_inc(logit_done, 1)

            def per_expert(ap):
                n = ap.shape[1]
                return ap.rearrange("p (n o) -> p n o", o=1).broadcast_to([P, n, E])

            def chained(instruction):
                dve.wait_ge(dve_step, signal(instruction))

            def route_scores(part):
                at = ROUTE_TILES[part]
                dve.wait_ge(sig_exp, part + 1)
                chained(nc.vector.tensor_scalar(score[:, at], score[:, at], 1.0, None, ALU.add))
                chained(nc.vector.reciprocal(score[:, at], score[:, at]))

            def route_pick(part, n):
                at, pick = ROUTE_TILES[part], (pick1, pick2)[n]
                top, who = best[:, n, at], best[:, 2, at]
                count = down_count[:, :].rearrange("p (o e) -> p o e", o=1).broadcast_to([P, at.stop - at.start, E])
                chained(nc.vector.tensor_reduce(top, score[:, at], AX_X, ALU.max))
                chained(nc.vector.tensor_tensor(tie[:, at], score[:, at], per_expert(top), ALU.is_equal))
                chained(nc.vector.tensor_tensor(tie[:, at], tie[:, at], count, ALU.mult))
                chained(nc.vector.tensor_reduce(who, tie[:, at], AX_X, ALU.max))
                chained(nc.vector.tensor_tensor(pick[:, at], tie[:, at], per_expert(who), ALU.is_equal))
                if n == 0:
                    chained(nc.vector.scalar_tensor_tensor(out=score[:, at], in0=pick[:, at], scalar=-4.0,
                                                           in1=score[:, at], op0=ALU.mult, op1=ALU.add))

            def route_weights(part):
                at = ROUTE_TILES[part]
                chained(nc.vector.tensor_tensor(best[:, 2, at], best[:, 0, at], best[:, 1, at], ALU.add))
                chained(nc.vector.tensor_scalar(best[:, 2, at], best[:, 2, at], 1e-6, None, ALU.add))
                chained(nc.vector.reciprocal(best[:, 3, at], best[:, 2, at]))
                for n in range(2):
                    last = nc.vector.tensor_tensor(best[:, n, at], best[:, n, at], best[:, 3, at], ALU.mult)
                chained(last)
                for n, pick in enumerate((pick1, pick2)):
                    last = nc.vector.tensor_tensor(pick[:, at], pick[:, at], per_expert(best[:, n, at]), ALU.mult)
                chained(last)
                nc.vector.tensor_tensor(weight.rearrange("p (n e) -> p n e", e=E)[:, at], pick1[:, at], pick2[:, at],
                                        ALU.add).then_inc(weight_ready, 1)

            def route(part, stage):
                if stage == 0:
                    route_scores(part)
                elif stage < 3:
                    route_pick(part, stage - 1)
                else:
                    route_weights(part)

            def split(u, par, helped=False):
                for h in range(FC // 2):
                    at = slice(h * 2 * BLOCK, (h + 1) * 2 * BLOCK)
                    dve.wait_ge(gelu_done, FC * u + 2 * h + 2)
                    if h == 0 and not (isinstance(u, int) and u < 2):
                        dve.wait_ge(down_done, u - 1)
                    if helped and h == 1:
                        dve.wait_ge(a_hi_act, u + 1)
                    else:
                        chunk = u + 1 if helped else 2 * u + h + 1 - NBLK
                        nc.vector.tensor_copy(a_hi[:, par, at], a_sb[:, par, at]).then_inc(a_hi_done, 1)
                        dve.wait_ge(a_hi_done, chunk)
                    nc.vector.tensor_tensor(a_lo[:, par, at], a_sb[:, par, at], a_hi[:, par, at].bitcast(F32),
                                            ALU.subtract).then_inc(a_lo_done, 1)

            def weigh(u, par, blk, n_slot, shared):
                dve.wait_ge(down_done, u + 1)
                bias = cols[:, bass.ds(n_slot + ROW_BD, 1)]
                if shared:
                    nc.vector.tensor_scalar(acc[:, bass.ds(blk * BLOCK, BLOCK)], bank[Y_BANK[par]][:, :], bias, 0.1,
                                            ALU.add, ALU.mult).then_inc(yw_ready, 1)
                else:
                    if not (isinstance(u, int) and u < NBLK + 2):
                        dve.wait_ge(acc_done, START + u - NBLK - 1)
                    w = w_bc[:, :, :].rearrange("p b t -> p (b t)")[:, bass.ds(blk * BLOCK, BLOCK)]
                    nc.vector.scalar_tensor_tensor(out=yw[:, par, :], in0=bank[Y_BANK[par]][:, :], scalar=bias, in1=w,
                                                   op0=ALU.add, op1=ALU.mult).then_inc(yw_ready, 1)

            def slot(s, base, n_slot, prefetch, after_shared=False):
                split(base, 0)
                weigh(base - 1, 1, NBLK - 1, n_slot - 1, after_shared)
                split(base + 1, 1)
                dve.wait_ge(w_bc_in[0], n_slot * 16)
                weigh(base, 0, 0, n_slot, False)
                if prefetch:
                    weights_lo(s + 1, n_slot + 1)
                with dve.Fori(1, NBLK // 2) as it:
                    split(base + it * 2, 0)
                    weigh(base + it * 2 - 1, 1, it * 2 - 1, n_slot, False)
                    dve.wait_ge(w_bc_in[1], n_slot * 16)
                    split(base + it * 2 + 1, 1)
                    weigh(base + it * 2, 0, it * 2, n_slot, False)

            def shared_unit(n):
                split(n, n % 2, True)
                if n > 0:
                    weigh(n - 1, (n - 1) % 2, n - 1, 0, True)

            for i in range(FIRST_STEP, STEPS):
                r = added_in(i)
                if r is not None:
                    dve.wait_ge(exp_done, CHUNK[2 * r + 2])
                    parts = exp_sum[:, 2 * r:2 * r + 2, 0:len(chunks(2 * r))]
                    count_of["row_sum", r] = signal(nc.vector.reduce_sum(row_sum[:, :], parts, AX_X))
                if phase(i, X_T) is not None:
                    h_low(phase(i, X_T))
                if phase(i, X_QK) is not None:
                    qk_low(phase(i, X_QK))
                if 0 <= i < TILES:
                    row_max(i)
                if phase(i, X_NORM) is not None:
                    x_norm(phase(i, X_NORM))
                if second(i, Y_NORM) is not None:
                    x2_norm(second(i, Y_NORM))
                if r is not None:
                    dve.wait_ge(dve_step, count_of["row_sum", r])
                    count_of["row_inv", r] = signal(nc.vector.reciprocal(row_inv[:, :], row_sum[:, :]))
                if phase(i, X_STATS) is not None:
                    x_statistics(phase(i, X_STATS))
                if r is not None:
                    residual(r)
                if second(i, Y_STATS) is not None:
                    x2_statistics(second(i, Y_STATS))
                if phase(i, X_STATS) is not None:
                    take_moments(("x", phase(i, X_STATS)))
                if second(i, Y_GATE) is not None:
                    logits_out(second(i, Y_GATE))
                t = turned_in(i)
                if t is not None:
                    for k in chunks(t):
                        if not on_act(CHUNK[t] + k):
                            probs_out(t, k)
                if second(i, Y_STATS) is not None:
                    take_moments(("y", second(i, Y_STATS)))
                s = weights_in(i)
                if s is not None:
                    weights_lo(s, s, lambda j: bank[SLOT["w", s, j] % RING])
                if i == FIRST_STEP:
                    silu_of_c()
                if i == STARTS[0] - 1:
                    first_mods()
                    projection_weights()
                if i - ROUTE_AT in range(4):
                    route(0, i - ROUTE_AT)
                if i == STARTS[0] + X_QK:
                    columns()
                    other_mods()
                if i in SHARED_AT:
                    shared_unit(SHARED_AT.index(i))

            for n in range(len(SHARED_AT), NBLK):
                if n == NBLK - 1:
                    dve.wait_ge(weightT_mm, 1)
                    for b in range(NB):
                        nc.vector.tensor_copy(weightT[:, b, :], bank[6][:, b * P:(b + 1) * P]).then_inc(weightT_ready, 1)
                shared_unit(n)
                if n == len(SHARED_AT):
                    route(1, 0)
                    route(1, 1)
                elif n == len(SHARED_AT) + 1:
                    route(1, 2)
                    route(1, 3)
            slot(1, NBLK, 1, True, after_shared=True)
            with dve.Fori(0, (SLOTS - 3) // 2) as pair:
                for par in (2, 3):
                    slot(par, (pair * 2 + par) * NBLK, pair * 2 + par, True)

            def add_sum(n):
                dve.wait_ge(accT_done, n + 1)
                at = slice(n * BLOCK, (n + 1) * BLOCK)
                nc.vector.tensor_tensor(x_sb[:, at], bank[5 + n % 2][:, :], x_sb[:, at], ALU.add).then_inc(out_ready, 1)

            base, n_slot = (SLOTS - 1) * NBLK, SLOTS - 1
            for n in range(NBLK):
                split(base + n, n % 2)
                if n % NQ == 1:
                    dve.wait_ge(w_bc_in[n // NQ], n_slot * 16)
                weigh(base + n - 1, (n - 1) % 2, (n - 1) % NBLK, n_slot if n else n_slot - 1, False)
                if n >= SUM_LAG:
                    add_sum(n - SUM_LAG)
            weigh(base + NBLK - 1, 1, NBLK - 1, n_slot, False)
            for n in range(NBLK - SUM_LAG, NBLK):
                add_sum(n)


_INS = ['L0_attn_x', 'L0_attn_Wk', 'L0_attn_Wq', 'L0_attn_Wv', 'L0_ffn_gate_w', 'L0_ffn_gate_bias', 'L0_ffn_Wu',
        'L0_ffn_bu', 'L0_ffn_Wd', 'L0_ffn_bd', 'L0_ffn_sWu', 'L0_ffn_sbu', 'L0_ffn_sWd', 'L0_ffn_sbd', 'L0_c', 'L0_wmod']


def kernel(**inputs):
    import numpy as _np
    import concourse.bacc as _bacc
    from concourse import mybir as _mybir
    from concourse.bass_utils import run_bass_kernel_spmd as _run

    nc = _bacc.Bacc("TRN2", target_bir_lowering=False, num_devices=1)
    arrays, args = {}, []
    for name in _INS:
        a = _np.ascontiguousarray(inputs[name])
        arrays[f"in_{name}_dram"] = a
        args.append(nc.dram_tensor(f"in_{name}_dram", a.shape, _mybir.dt.from_np(a.dtype), kind="ExternalInput").ap())
    shape = inputs["L0_attn_x"].shape
    args.append(nc.dram_tensor("out_0_dram", shape, _mybir.dt.float32, kind="ExternalOutput").ap())
    adaln_attention_moe(nc, *args)
    r = _run(nc, [arrays], core_ids=[0])
    return r.results[0]["out_0_dram"]
```
